# Optimizing a Trainium2 kernel written in Bass

```python
import numpy as np
import jax
import jax.numpy as jnp

def _softmax(x, axis=-1):
    return jax.nn.softmax(x, axis=axis)

def _gelu(x):
    return jax.nn.gelu(x, approximate=True)

def _silu(x):
    return jax.nn.silu(x)

def _sigmoid(x):
    return jax.nn.sigmoid(x)

def _layernorm(x, axis=-1, eps=1e-05):
    m = jnp.mean(x, axis=axis, keepdims=True)
    v = jnp.var(x, axis=axis, keepdims=True)
    return (x - m) / jnp.sqrt(v + eps)

def _scatter_add(tgt, idx, src, axis=0):
    return tgt.at[idx].add(src)

def _segment_sum(src, seg, n):
    return jax.ops.segment_sum(src, seg, n)
kernel_name = 'mk_seq_preln_d1_jaxref_r8_92c32f'

def setup_inputs(seed: int=0):
    np.random.seed(seed)
    _w = jnp.asarray

    def _L0_attn_setup():
        import jax, jax.numpy as jnp
        import numpy as np
        B, L = (2, 256)
        D_MODEL = 128
        D_STATE = 128
        D_CONV = 4
        EXPAND = 2
        HEADDIM = 64
        D_HALF = D_MODEL // 2
        D_INNER = EXPAND * D_HALF
        NHEADS = D_INNER // HEADDIM
        CONV_DIM = D_INNER + 2 * D_STATE
        D_IN_PROJ = 2 * D_INNER + 2 * D_STATE + NHEADS
        EPS = 1e-05

        def _rmsnorm(x, w):
            return x * jax.lax.rsqrt(jnp.mean(x * x, axis=-1, keepdims=True) + EPS) * w

        def _mamba2(u, in_w, conv_w, conv_b, dt_bias, A_log, D, gnorm_w, outp_w):
            b, l, _ = u.shape
            zxbcdt = u @ in_w.T
            z = zxbcdt[..., :D_INNER]
            xBC = zxbcdt[..., D_INNER:D_INNER + CONV_DIM]
            dt = zxbcdt[..., D_INNER + CONV_DIM:]
            xp = jnp.pad(xBC, ((0, 0), (D_CONV - 1, 0), (0, 0)))
            conv = conv_b + sum((xp[:, k:k + l, :] * conv_w[:, k] for k in range(D_CONV)))
            xBC = jax.nn.silu(conv)
            x = xBC[..., :D_INNER]
            Bm = xBC[..., D_INNER:D_INNER + D_STATE]
            Cm = xBC[..., D_INNER + D_STATE:]
            dt = jax.nn.softplus(dt + dt_bias)
            A = -jnp.exp(A_log)
            xh = x.reshape(b, l, NHEADS, HEADDIM)
            dA = jnp.exp(dt * A)
            dtx = dt[..., None] * xh

            def step(h, inp):
                dA_t, dtx_t, B_t, C_t = inp
                h = dA_t[:, :, None, None] * h + jnp.einsum('bhp,bn->bhpn', dtx_t, B_t)
                return (h, jnp.einsum('bhpn,bn->bhp', h, C_t))
            h0 = jnp.zeros((b, NHEADS, HEADDIM, D_STATE), u.dtype)
            xs = (jnp.moveaxis(dA, 1, 0), jnp.moveaxis(dtx, 1, 0), jnp.moveaxis(Bm, 1, 0), jnp.moveaxis(Cm, 1, 0))
            _, ys = jax.lax.scan(step, h0, xs)
            y = jnp.moveaxis(ys, 0, 1) + xh * D[None, None, :, None]
            y = y.reshape(b, l, D_INNER) * jax.nn.silu(z)
            y = _rmsnorm(y, gnorm_w)
            return y @ outp_w.T

        def _forward(x, norm_w, op_w, op_b, f_in_w, f_conv_w, f_conv_b, f_dt_bias, f_A_log, f_D, f_gnorm_w, f_outp_w, b_in_w, b_conv_w, b_conv_b, b_dt_bias, b_A_log, b_D, b_gnorm_w, b_outp_w):
            xn = _rmsnorm(x, norm_w)
            x_f, x_b = (xn[..., :D_HALF], xn[..., D_HALF:])
            out_f = _mamba2(x_f, f_in_w, f_conv_w, f_conv_b, f_dt_bias, f_A_log, f_D, f_gnorm_w, f_outp_w)
            out_b = jnp.flip(_mamba2(jnp.flip(x_b, 1), b_in_w, b_conv_w, b_conv_b, b_dt_bias, b_A_log, b_D, b_gnorm_w, b_outp_w), 1)
            out = jnp.concatenate([out_f, out_b], axis=-1) @ op_w.T + op_b
            return x + out

        def _mamba_params(key, prefix):
            k = jax.random.split(key, 5)
            return {prefix + 'in_w': jax.random.normal(k[0], (D_IN_PROJ, D_HALF), jnp.float32) * 0.02, prefix + 'conv_w': jax.random.normal(k[1], (CONV_DIM, D_CONV), jnp.float32) * 0.2, prefix + 'conv_b': jnp.zeros((CONV_DIM,), jnp.float32), prefix + 'dt_bias': jax.random.normal(k[2], (NHEADS,), jnp.float32) * 0.1, prefix + 'A_log': jnp.log(jax.random.uniform(k[3], (NHEADS,), jnp.float32, 1.0, 16.0)), prefix + 'D': jnp.ones((NHEADS,), jnp.float32), prefix + 'gnorm_w': jnp.ones((D_INNER,), jnp.float32), prefix + 'outp_w': jax.random.normal(k[4], (D_HALF, D_INNER), jnp.float32) * 0.02}
        key = jax.random.key(seed)
        k = jax.random.split(key, 4)
        inp = {'x': jax.random.normal(k[0], (B, L, D_MODEL), jnp.float32), 'norm_w': jnp.ones((D_MODEL,), jnp.float32), 'op_w': jax.random.normal(k[1], (D_MODEL, D_MODEL), jnp.float32) * 0.02, 'op_b': jnp.zeros((D_MODEL,), jnp.float32)}
        inp.update(_mamba_params(k[2], 'f_'))
        inp.update(_mamba_params(k[3], 'b_'))
        return inp
    _L0_attn_in = _L0_attn_setup()

    def _L0_ffn_setup():
        import jax, jax.numpy as jnp
        import numpy as np
        H = 128
        I = 88
        E = 64
        TOP_K = 8
        NG = 8
        TOPK_GROUP = 4
        N_SHARED = 2
        ROUTED_SCALE = 2.5
        S_I = I * N_SHARED

        def _route(x, gate_w, gate_bias):
            T = x.shape[0]
            logits = x @ gate_w.T
            scores = jax.nn.sigmoid(logits)
            scores_for_choice = scores + gate_bias[None, :]
            grp = scores_for_choice.reshape(T, NG, E // NG)
            group_scores = jnp.sum(jax.lax.top_k(grp, 2)[0], axis=-1)
            _, gidx = jax.lax.top_k(group_scores, TOPK_GROUP)
            gmask = jnp.zeros((T, NG), dtype=scores.dtype).at[jnp.arange(T)[:, None], gidx].set(1.0)
            emask = jnp.repeat(gmask, E // NG, axis=1)
            masked = jnp.where(emask > 0, scores_for_choice, 0.0)
            _, topk_idx = jax.lax.top_k(masked, TOP_K)
            topk_w = jnp.take_along_axis(scores, topk_idx, axis=1)
            topk_w = topk_w / (jnp.sum(topk_w, axis=-1, keepdims=True) + 1e-20)
            topk_w = topk_w * ROUTED_SCALE
            rw = jnp.zeros((T, E), dtype=scores.dtype).at[jnp.arange(T)[:, None], topk_idx].add(topk_w)
            return rw

        def _mlp(x, gw, uw, dw):
            return jax.nn.silu(x @ gw.T) * (x @ uw.T) @ dw.T
        key = jax.random.key(seed)
        ks = jax.random.split(key, 10)
        sc = 0.02
        return {'hidden_states': jax.random.normal(ks[0], (1, 128, H), dtype=jnp.float32), 'gate_w': sc * jax.random.normal(ks[1], (E, H), dtype=jnp.float32), 'gate_bias': sc * jax.random.normal(ks[2], (E,), dtype=jnp.float32), 'Wg': sc * jax.random.normal(ks[3], (E, I, H), dtype=jnp.float32), 'Wu': sc * jax.random.normal(ks[4], (E, I, H), dtype=jnp.float32), 'Wd': sc * jax.random.normal(ks[5], (E, H, I), dtype=jnp.float32), 'Sg': sc * jax.random.normal(ks[6], (S_I, H), dtype=jnp.float32), 'Su': sc * jax.random.normal(ks[7], (S_I, H), dtype=jnp.float32), 'Sd': sc * jax.random.normal(ks[8], (H, S_I), dtype=jnp.float32)}
    _L0_ffn_in = _L0_ffn_setup()
    _d = {'L0_attn_x': _L0_attn_in['x'], 'L0_attn_norm_w': _L0_attn_in['norm_w'], 'L0_attn_op_w': _L0_attn_in['op_w'], 'L0_attn_op_b': _L0_attn_in['op_b'], 'L0_attn_f_in_w': _L0_attn_in['f_in_w'], 'L0_attn_f_conv_w': _L0_attn_in['f_conv_w'], 'L0_attn_f_conv_b': _L0_attn_in['f_conv_b'], 'L0_attn_f_dt_bias': _L0_attn_in['f_dt_bias'], 'L0_attn_f_A_log': _L0_attn_in['f_A_log'], 'L0_attn_f_D': _L0_attn_in['f_D'], 'L0_attn_f_gnorm_w': _L0_attn_in['f_gnorm_w'], 'L0_attn_f_outp_w': _L0_attn_in['f_outp_w'], 'L0_attn_b_in_w': _L0_attn_in['b_in_w'], 'L0_attn_b_conv_w': _L0_attn_in['b_conv_w'], 'L0_attn_b_conv_b': _L0_attn_in['b_conv_b'], 'L0_attn_b_dt_bias': _L0_attn_in['b_dt_bias'], 'L0_attn_b_A_log': _L0_attn_in['b_A_log'], 'L0_attn_b_D': _L0_attn_in['b_D'], 'L0_attn_b_gnorm_w': _L0_attn_in['b_gnorm_w'], 'L0_attn_b_outp_w': _L0_attn_in['b_outp_w'], 'L0_ffn_gate_w': _L0_ffn_in['gate_w'], 'L0_ffn_gate_bias': _L0_ffn_in['gate_bias'], 'L0_ffn_Wg': _L0_ffn_in['Wg'], 'L0_ffn_Wu': _L0_ffn_in['Wu'], 'L0_ffn_Wd': _L0_ffn_in['Wd'], 'L0_ffn_Sg': _L0_ffn_in['Sg'], 'L0_ffn_Su': _L0_ffn_in['Su'], 'L0_ffn_Sd': _L0_ffn_in['Sd']}
    _x0 = _d['L0_attn_x']
    _d['L0_attn_x'] = jax.random.normal(jax.random.fold_in(jax.random.key(seed), 1), (16, 256, 128), dtype=_x0.dtype)
    del _x0
    return _d

def reference(L0_attn_x, L0_attn_norm_w, L0_attn_op_w, L0_attn_op_b, L0_attn_f_in_w, L0_attn_f_conv_w, L0_attn_f_conv_b, L0_attn_f_dt_bias, L0_attn_f_A_log, L0_attn_f_D, L0_attn_f_gnorm_w, L0_attn_f_outp_w, L0_attn_b_in_w, L0_attn_b_conv_w, L0_attn_b_conv_b, L0_attn_b_dt_bias, L0_attn_b_A_log, L0_attn_b_D, L0_attn_b_gnorm_w, L0_attn_b_outp_w, L0_ffn_gate_w, L0_ffn_gate_bias, L0_ffn_Wg, L0_ffn_Wu, L0_ffn_Wd, L0_ffn_Sg, L0_ffn_Su, L0_ffn_Sd):

    def _L0_attn_ref(x, norm_w, op_w, op_b, f_in_w, f_conv_w, f_conv_b, f_dt_bias, f_A_log, f_D, f_gnorm_w, f_outp_w, b_in_w, b_conv_w, b_conv_b, b_dt_bias, b_A_log, b_D, b_gnorm_w, b_outp_w):
        import jax, jax.numpy as jnp
        import numpy as np
        B, L = (2, 256)
        D_MODEL = 128
        D_STATE = 128
        D_CONV = 4
        EXPAND = 2
        HEADDIM = 64
        D_HALF = D_MODEL // 2
        D_INNER = EXPAND * D_HALF
        NHEADS = D_INNER // HEADDIM
        CONV_DIM = D_INNER + 2 * D_STATE
        D_IN_PROJ = 2 * D_INNER + 2 * D_STATE + NHEADS
        EPS = 1e-05

        def _rmsnorm(x, w):
            return x * jax.lax.rsqrt(jnp.mean(x * x, axis=-1, keepdims=True) + EPS) * w

        def _mamba2(u, in_w, conv_w, conv_b, dt_bias, A_log, D, gnorm_w, outp_w):
            b, l, _ = u.shape
            zxbcdt = u @ in_w.T
            z = zxbcdt[..., :D_INNER]
            xBC = zxbcdt[..., D_INNER:D_INNER + CONV_DIM]
            dt = zxbcdt[..., D_INNER + CONV_DIM:]
            xp = jnp.pad(xBC, ((0, 0), (D_CONV - 1, 0), (0, 0)))
            conv = conv_b + sum((xp[:, k:k + l, :] * conv_w[:, k] for k in range(D_CONV)))
            xBC = jax.nn.silu(conv)
            x = xBC[..., :D_INNER]
            Bm = xBC[..., D_INNER:D_INNER + D_STATE]
            Cm = xBC[..., D_INNER + D_STATE:]
            dt = jax.nn.softplus(dt + dt_bias)
            A = -jnp.exp(A_log)
            xh = x.reshape(b, l, NHEADS, HEADDIM)
            dA = jnp.exp(dt * A)
            dtx = dt[..., None] * xh

            def step(h, inp):
                dA_t, dtx_t, B_t, C_t = inp
                h = dA_t[:, :, None, None] * h + jnp.einsum('bhp,bn->bhpn', dtx_t, B_t)
                return (h, jnp.einsum('bhpn,bn->bhp', h, C_t))
            h0 = jnp.zeros((b, NHEADS, HEADDIM, D_STATE), u.dtype)
            xs = (jnp.moveaxis(dA, 1, 0), jnp.moveaxis(dtx, 1, 0), jnp.moveaxis(Bm, 1, 0), jnp.moveaxis(Cm, 1, 0))
            _, ys = jax.lax.scan(step, h0, xs)
            y = jnp.moveaxis(ys, 0, 1) + xh * D[None, None, :, None]
            y = y.reshape(b, l, D_INNER) * jax.nn.silu(z)
            y = _rmsnorm(y, gnorm_w)
            return y @ outp_w.T

        def _forward(x, norm_w, op_w, op_b, f_in_w, f_conv_w, f_conv_b, f_dt_bias, f_A_log, f_D, f_gnorm_w, f_outp_w, b_in_w, b_conv_w, b_conv_b, b_dt_bias, b_A_log, b_D, b_gnorm_w, b_outp_w):
            xn = _rmsnorm(x, norm_w)
            x_f, x_b = (xn[..., :D_HALF], xn[..., D_HALF:])
            out_f = _mamba2(x_f, f_in_w, f_conv_w, f_conv_b, f_dt_bias, f_A_log, f_D, f_gnorm_w, f_outp_w)
            out_b = jnp.flip(_mamba2(jnp.flip(x_b, 1), b_in_w, b_conv_w, b_conv_b, b_dt_bias, b_A_log, b_D, b_gnorm_w, b_outp_w), 1)
            out = jnp.concatenate([out_f, out_b], axis=-1) @ op_w.T + op_b
            return x + out

        def _mamba_params(key, prefix):
            k = jax.random.split(key, 5)
            return {prefix + 'in_w': jax.random.normal(k[0], (D_IN_PROJ, D_HALF), jnp.float32) * 0.02, prefix + 'conv_w': jax.random.normal(k[1], (CONV_DIM, D_CONV), jnp.float32) * 0.2, prefix + 'conv_b': jnp.zeros((CONV_DIM,), jnp.float32), prefix + 'dt_bias': jax.random.normal(k[2], (NHEADS,), jnp.float32) * 0.1, prefix + 'A_log': jnp.log(jax.random.uniform(k[3], (NHEADS,), jnp.float32, 1.0, 16.0)), prefix + 'D': jnp.ones((NHEADS,), jnp.float32), prefix + 'gnorm_w': jnp.ones((D_INNER,), jnp.float32), prefix + 'outp_w': jax.random.normal(k[4], (D_HALF, D_INNER), jnp.float32) * 0.02}
        return _forward(x, norm_w, op_w, op_b, f_in_w, f_conv_w, f_conv_b, f_dt_bias, f_A_log, f_D, f_gnorm_w, f_outp_w, b_in_w, b_conv_w, b_conv_b, b_dt_bias, b_A_log, b_D, b_gnorm_w, b_outp_w)

    def _L0_ffn_ref(hidden_states, gate_w, gate_bias, Wg, Wu, Wd, Sg, Su, Sd):
        import jax, jax.numpy as jnp
        import numpy as np
        H = 128
        I = 88
        E = 64
        TOP_K = 8
        NG = 8
        TOPK_GROUP = 4
        N_SHARED = 2
        ROUTED_SCALE = 2.5
        S_I = I * N_SHARED

        def _route(x, gate_w, gate_bias):
            T = x.shape[0]
            logits = x @ gate_w.T
            scores = jax.nn.sigmoid(logits)
            scores_for_choice = scores + gate_bias[None, :]
            grp = scores_for_choice.reshape(T, NG, E // NG)
            group_scores = jnp.sum(jax.lax.top_k(grp, 2)[0], axis=-1)
            _, gidx = jax.lax.top_k(group_scores, TOPK_GROUP)
            gmask = jnp.zeros((T, NG), dtype=scores.dtype).at[jnp.arange(T)[:, None], gidx].set(1.0)
            emask = jnp.repeat(gmask, E // NG, axis=1)
            masked = jnp.where(emask > 0, scores_for_choice, 0.0)
            _, topk_idx = jax.lax.top_k(masked, TOP_K)
            topk_w = jnp.take_along_axis(scores, topk_idx, axis=1)
            topk_w = topk_w / (jnp.sum(topk_w, axis=-1, keepdims=True) + 1e-20)
            topk_w = topk_w * ROUTED_SCALE
            rw = jnp.zeros((T, E), dtype=scores.dtype).at[jnp.arange(T)[:, None], topk_idx].add(topk_w)
            return rw

        def _mlp(x, gw, uw, dw):
            return jax.nn.silu(x @ gw.T) * (x @ uw.T) @ dw.T
        B, S, _ = hidden_states.shape
        x = hidden_states.reshape(B * S, H)
        rw = _route(x, gate_w, gate_bias)
        expert_out = jax.vmap(lambda gw_, uw_, dw_: _mlp(x, gw_, uw_, dw_))(Wg, Wu, Wd)
        routed = jnp.einsum('eth,te->th', expert_out, rw)
        shared = _mlp(x, Sg, Su, Sd)
        out = (routed + shared).reshape(B, S, H)
        return out
    x = L0_attn_x
    x = x + _L0_attn_ref(_layernorm(x, axis=-1), L0_attn_norm_w, L0_attn_op_w, L0_attn_op_b, L0_attn_f_in_w, L0_attn_f_conv_w, L0_attn_f_conv_b, L0_attn_f_dt_bias, L0_attn_f_A_log, L0_attn_f_D, L0_attn_f_gnorm_w, L0_attn_f_outp_w, L0_attn_b_in_w, L0_attn_b_conv_w, L0_attn_b_conv_b, L0_attn_b_dt_bias, L0_attn_b_A_log, L0_attn_b_D, L0_attn_b_gnorm_w, L0_attn_b_outp_w)
    x = x + _L0_ffn_ref(_layernorm(x, axis=-1), L0_ffn_gate_w, L0_ffn_gate_bias, L0_ffn_Wg, L0_ffn_Wu, L0_ffn_Wd, L0_ffn_Sg, L0_ffn_Su, L0_ffn_Sd)
    return x

_drawn_inputs = setup_inputs


def setup_inputs(seed=0):
    import zlib

    import numpy as np

    out = dict(_drawn_inputs(seed))
    spreads = {'L0_attn_norm_w': (1.0, 0.6),
     'L0_attn_op_b': (0.0, 0.1),
     'L0_attn_f_conv_b': (0.0, 0.591),
     'L0_attn_f_D': (1.0, 0.6),
     'L0_attn_f_gnorm_w': (1.0, 0.6),
     'L0_attn_b_conv_b': (0.0, 0.693),
     'L0_attn_b_D': (1.0, 0.6),
     'L0_attn_b_gnorm_w': (1.0, 0.6)}
    factors = {'L0_attn_op_w': 2.676,
     'L0_attn_f_in_w': 3.513,
     'L0_attn_f_conv_w': 6.742,
     'L0_attn_f_dt_bias': 8.0,
     'L0_attn_f_A_log': 8.0,
     'L0_attn_f_outp_w': 3.633,
     'L0_attn_b_in_w': 3.984,
     'L0_attn_b_conv_w': 6.465,
     'L0_attn_b_dt_bias': 8.0,
     'L0_attn_b_A_log': 8.0,
     'L0_attn_b_outp_w': 3.92,
     'L0_ffn_gate_w': 8.0,
     'L0_ffn_gate_bias': 8.0,
     'L0_ffn_Wg': 8.0,
     'L0_ffn_Wu': 8.0,
     'L0_ffn_Wd': 8.0,
     'L0_ffn_Sg': 8.0,
     'L0_ffn_Su': 8.0,
     'L0_ffn_Sd': 8.0}
    for name, (base, spread) in spreads.items():
        noise = np.random.default_rng([zlib.crc32(name.encode()), seed]).standard_normal(out[name].shape)
        drawn = base * np.exp(spread * noise) if base else spread * noise
        out[name] = jnp.asarray(drawn.astype(out[name].dtype))
    for name, factor in factors.items():
        out[name] = (out[name] * factor).astype(out[name].dtype)
    return out
```

```python
from contextlib import ExitStack

import concourse.bass as bass
from concourse import mybir

F32 = mybir.dt.float32
F32R = mybir.dt.float32r
ALU = mybir.AluOpType
ACT = mybir.ActivationFunctionType
X = mybir.AxisListType.X

P = 128
B, L, C = 16, 256, 128
T = B * L
HALF = C // 2
JT = L // P
NT = T // P
NHD = 2
HD = 64
LB = L + P
KCONV = 4
E, I, TOPK, NG, TOPG, SCALE = 64, 88, 8, 8, 4, 2.5
EPG = E // NG
SI = 2 * I
RC = E * I // P
SC = -(-SI // P)
NC = RC + SC
TB = 512
NB = T // TB
BT = TB // P
WCOLS = 3 * NC * P
WSTEP = WCOLS // (2 * B)
LAG = 3
HS = 256
EPS = 1e-5
TAPS = (((3, 2), (1, 0)), ((2, 3), (0, 1)))
LOWEST = -3.0e38
NCOL = 2 * (3 * KCONV + 3) + 7 + 4
CW, CB = (0, 15), (12, 27)
NWS = (30, 31)
NWN = 32
DCOL = (33, 34)
GN = (35, 36)
WDT = 37
ROW_DTB, ROW_ALOG, ROW_OPB, ROW_GB, NROW = 0, 4, 8, 8 + C, 8 + C + E
K_SCAN, K_TRI, NK = 0, LB, LB + NG * NG


def bidirectional_mamba_moe(nc, x_d, cols_d, rows_d, inw_d, mo_d, gwt_d, wall_d, const_d, out_d):
    decay_d = nc.dram_tensor("decay_scratch", (2 * NHD, T), F32, kind="Internal").ap()
    x2_d = nc.dram_tensor("x2_scratch", (T, C), F32, kind="Internal").ap()

    with ExitStack() as ctx:
        def sb(name, shape, dt=F32):
            return ctx.enter_context(nc.sbuf_tensor(name, shape, dt))

        def sem(name):
            return ctx.enter_context(nc.semaphore(name))

        w_hi = sb("w_hi", [P, WCOLS], F32R)
        w_lo = sb("w_lo", [P, WCOLS], F32R)
        w_stage = sb("w_stage", [P, 2, WSTEP])
        x3_hi = [sb(f"x3_hi{i}", [P, TB], F32R) for i in range(2)]
        x3_lo = [sb(f"x3_lo{i}", [P, TB], F32R) for i in range(2)]
        h_hi = [sb(f"h_hi{i}", [P, TB], F32R) for i in range(2)]
        h_lo = [sb(f"h_lo{i}", [P, TB], F32R) for i in range(2)]
        gw_hi = sb("gw_hi", [P, E], F32R)
        gw_lo = sb("gw_lo", [P, E], F32R)
        scan_eye = sb("scan_eye", [P, LB])
        ident = scan_eye[:, 0:P]
        tri = sb("tri", [P, NG * NG])
        rows = sb("rows", [P, NROW])
        half_neg = sb("half_neg", [P, NT])
        eps_t = sb("eps_t", [P, BT])
        ones = sb("ones", [P, 1])

        ARENA = 11850
        arena = sb("arena", [P, ARENA])
        used = [0]

        def cut(*shape):
            n = 1
            for s in shape:
                n *= s
            at = used[0]
            used[0] += n
            assert used[0] <= ARENA, used[0]
            v = arena[:, at:at + n]
            if len(shape) == 2:
                return v.rearrange("p (a b) -> p a b", a=shape[0])
            if len(shape) == 3:
                return v.rearrange("p (a b c) -> p a b c", a=shape[0], b=shape[1])
            return v

        cols = cut(NCOL)
        wproj = cut(2, 7, P)
        mo_w = cut(2, P)
        dt_all = cut(NT, 2 * NHD)
        c1 = cut(NT)
        c2 = cut(NT)
        mean_rms = cut(NT, 2)
        at_xt = used[0]
        xt = [cut(JT, C) for _ in range(2)]
        base = [cut(JT, C) for _ in range(2)]
        at_u2 = used[0]
        u2 = cut(JT, 2 * C)
        at_stack = used[0]
        stack = [[cut(L + 4) for _ in range(2)] for _ in range(2)]
        szT1 = cut(L)
        shared = used[0]
        decay = [cut(NHD, LB) for _ in range(2)]
        at_ysqT = used[0]
        ysqT = [cut(L) for _ in range(2)]
        at_lmask = used[0]
        lmask = [cut(NHD, LB) for _ in range(2)]
        szT = [cut(L), szT1]
        at_xT = used[0]
        xT = [cut(L) for _ in range(2)]
        at_bT = used[0]
        bT = [cut(L) for _ in range(2)]
        cT = [cut(L) for _ in range(2)]
        at_xdt = used[0]
        xdt = [cut(JT, NHD, HD) for _ in range(2)]
        yT = [cut(L) for _ in range(2)]
        rms = cut(2 * JT)
        mamba_end = used[0]
        used[0] = shared
        x_ring = cut(4 * BT, C)
        wnat = cut(2, 7, P)
        inw = cut(2, 4, HALF)
        xT_pro = cut(2, TB)
        stats = cut(NT, 6)
        mv = cut(NT, 2)
        variance, root, newton, factor = (cut(2, NT) for _ in range(4))
        mo_sb = cut(4, P)
        gwt = cut(E)
        wdt = cut(2 * NHD)
        ea = cut(2 * NHD)
        sp_arg, sp_abs, sp_e, sp_s, sp_s2, sp_p = (wnat[:, 0, i, :] for i in range(6))
        decT = sp_s

        def x_block(n):
            if n in (4, 5):
                return w_stage[:, n - 4, 0:BT * C].rearrange("p (j c) -> p j c", j=BT)
            at = (n % 6) * BT
            return x_ring[:, at:at + BT, :]

        used[0] = at_u2
        x2t = cut(BT, C)
        used[0] = at_stack
        x3t = cut(BT, C)
        used[0] = shared
        nexp = cut(BT, E)
        scores = cut(BT, E)
        choice = cut(BT, E)
        masked = cut(BT, E)
        repl = cut(BT, E)
        wsel = cut(BT, E)
        assert used[0] <= at_ysqT
        used[0] = at_bT
        t1h, t1l = cut(BT * NG, 4), cut(BT * NG, 4)
        t2h, t2a, t2b, t2l = (cut(BT * NG, 2) for _ in range(4))
        t3h, t3a, t3b, gs = (cut(BT * NG, 1) for _ in range(4))
        assert used[0] <= at_xdt
        used[0] = at_lmask
        cmp1, cmp2 = cut(BT, NG * NG), cut(BT, NG * NG)
        rank = cut(BT, NG)
        m8 = cut(BT, 8)
        den = cut(BT)
        used[0] = at_lmask + NHD * LB
        rwp = cut(BT, 2 * E)
        used[0] = mamba_end
        st2 = cut(BT, 6)
        mv2 = cut(BT, 2)
        rs2 = cut(2, BT)
        used[0] = 0
        s_t = [cut(TB) for _ in range(2)]
        a_t = [cut(TB) for _ in range(2)]
        assert used[0] <= at_xt
        used[0] = at_xt
        h0 = cut(TB)
        h1 = cut(TB)
        h_t = [h0, h1]
        assert used[0] <= at_u2
        used[0] = at_stack + TB
        rwb0 = cut(TB)
        used[0] = at_ysqT
        rwb = [rwb0, cut(TB)]
        assert used[0] <= at_lmask
        used[0] = at_xT
        x2T0 = cut(TB)
        assert used[0] <= at_bT
        used[0] = at_xdt
        x2T = [x2T0, cut(TB)]
        ob = cut(TB)
        assert used[0] <= mamba_end

        bank = [ctx.enter_context(nc.psum_tensor(f"bank{i}", [P, 512], F32)) for i in range(8)]

        eye_in = sem("eye_in")
        inw_in = sem("inw_in")
        params_in = sem("params_in")
        x_all_in = [sem(f"x_all_in{i}") for i in range(NB)]
        init_done = sem("init_done")
        stats_ready = sem("stats_ready")
        mv_ready = sem("mv_ready")
        centered = sem("centered")
        variance_ready = sem("variance_ready")
        root_ready = sem("root_ready")
        norm_ready = sem("norm_ready")
        link_v = sem("link_v")
        wnat_ready = sem("wnat_ready")
        wnat1_ready = sem("wnat1_ready")
        wT_ready = sem("wT_ready")
        wT_copied = sem("wT_copied")
        mo_ready = sem("mo_ready")
        mo_copied = sem("mo_copied")
        wdt_ready = sem("wdt_ready")
        ea_ready = sem("ea_ready")
        xproT_ready = sem("xproT_ready")
        xproT_copied = sem("xproT_copied")
        dt_ready = sem("dt_ready")
        abs_ready = sem("abs_ready")
        e_ready = sem("e_ready")
        arg_ready = sem("arg_ready")
        dec_ready = sem("dec_ready")
        decT_ready = sem("decT_ready")
        decT_copied = sem("decT_copied")
        dec_out = sem("dec_out")
        gw_ready = sem("gw_ready")

        x_in = [sem(f"x_in{i}") for i in range(2)]
        decay_in = [sem(f"decay_in{i}") for i in range(2)]
        pads_ready = sem("pads_ready")
        u_ready = sem("u_ready")
        t_ready = sem("t_ready")
        stack_ready = sem("stack_ready")
        proj_ready = sem("proj_ready")
        silu_ready = sem("silu_ready")
        xtok_ready = sem("xtok_ready")
        g_ready = sem("g_ready")
        xdt_ready = sem("xdt_ready")
        l_ready = sem("l_ready")
        m_ready = sem("m_ready")
        y_ready = sem("y_ready")
        y1_ready = sem("y1_ready")
        y2_ready = sem("y2_ready")
        ysq_ready = sem("ysq_ready")
        ssq_ready = sem("ssq_ready")
        out_ready = sem("out_ready")
        msq_ready = sem("msq_ready")
        rms_ready = sem("rms_ready")
        base_half = sem("base_half")
        base_ready = sem("base_ready")
        x2_half = sem("x2_half")
        x2_ready = sem("x2_ready")
        x2_out = [sem(f"x2_out{i}") for i in range(2)]
        w_in = [sem(f"w_in{i}") for i in range(2)]
        whi_ready = sem("whi_ready")
        wlo_ready = sem("wlo_ready")
        mamba_over = sem("mamba_over")

        x2_in = sem("x2_in")
        stat2_ready = sem("stat2_ready")
        mv2_ready = sem("mv2_ready")
        rs2_half = sem("rs2_half")
        rs2_ready = sem("rs2_ready")
        x3_ready = sem("x3_ready")
        x3T_ready = sem("x3T_ready")
        x2T_ready = sem("x2T_ready")
        x3hi_ready = sem("x3hi_ready")
        x2T_copied = sem("x2T_copied")
        x3lo_ready = sem("x3lo_ready")
        logits_ready = sem("logits_ready")
        nexp_ready = sem("nexp_ready")
        route_link = sem("route_link")
        rwp_ready = sem("rwp_ready")
        rwT_ready = sem("rwT_ready")
        rwb_ready = sem("rwb_ready")
        up_ready = sem("up_ready")
        gate_ready = sem("gate_ready")
        s_ready = sem("s_ready")
        a_ready = sem("a_ready")
        hp_ready = sem("hp_ready")
        hv_ready = sem("hv_ready")
        hhi_ready = sem("hhi_ready")
        lop_ready = sem("lop_ready")
        lov_ready = sem("lov_ready")
        down_done = sem("down_done")
        ob_ready = sem("ob_ready")
        out_sent = sem("out_sent")

        block = ctx.enter_context(nc.Block())

        def sequences(eng, body):
            body(0, 0, 0)
            body(1, 0, 1)
            with eng.Fori(0, B // 2 - 2) as k:
                body(k * 2 + 2, k + 1, 0)
                body(k * 2 + 3, k + 1, 1)
            body(14, 7, 0)
            body(15, 7, 1)

        def blocks(eng, body):
            with eng.Fori(0, NB // 2 - 1) as k:
                body(k * 2, 0, True)
                body(k * 2 + 1, 1, True)
            body(NB - 2, 0, True)
            body(NB - 1, 1, False)

        def x3_bank(n):
            return 0 if isinstance(n, int) and n == 0 else 6

        def logit_bank(n):
            return 1 if isinstance(n, int) and n == 0 else 6

        def last(b, n):
            return isinstance(b, int) and b >= B - n

        def barrier(eng, s):
            eng.sem_inc(s, 1)
            eng.wait_ge(s, 5)

        def bc(ap, axis, n):
            v = ap.unsqueeze(axis)
            shape = list(v.shape)
            shape[axis] = n
            return v.to_broadcast(shape)

        @block.sync
        def _(sp):
            sp.dma_start(cols, cols_d).then_inc(inw_in, 16)
            sp.dma_start(inw, inw_d).then_inc(inw_in, 16)
            x_v = x_d.rearrange("(n p) c -> p n c", p=P)
            for n in range(NB):
                if n >= 6:
                    sp.wait_ge(xproT_ready, n - 5)
                sp.dma_start(x_block(n), x_v[:, BT * n:BT * n + BT, :]).then_inc(x_all_in[n], 16)
                if n == 0:
                    sp.dma_start(scan_eye[:, :], const_d[:, K_SCAN:K_SCAN + LB]).then_inc(eye_in, 16)
                if n == 5:
                    sp.dma_start(rows[:, :], rows_d.partition_broadcast(P).rearrange("p a c -> p (a c)")).then_inc(params_in, 16)
                    sp.dma_start(mo_sb[0:HALF, :, :], mo_d).then_inc(params_in, 16)
                    sp.dma_start(gwt, gwt_d).then_inc(params_in, 16)
                    sp.dma_start(tri[:, :], const_d[:, K_TRI:NK]).then_inc(params_in, 16)
            x_seq = x_d.rearrange("(b j p) c -> p b j c", p=P, j=JT)
            x2_seq = x2_d.rearrange("(b j p) c -> p b j c", p=P, j=JT)

            def load_x(b, par):
                sp.dma_start(xt[par], x_seq[:, bass.ds(b, 1), :, :].rearrange("p o j c -> p (o j) c")).then_inc(x_in[par], 16)

            def load_decay(b, d):
                spans = (((1, 1, L - 1), (L + 1, P + 1, P - 1)), ((0, 0, P - 1), (P, 0, L - 1)))[d]
                for col, t, n in spans:
                    src = decay_d[NHD * d:NHD * d + NHD, bass.ds(b * L + t, n)].partition_broadcast(P)
                    sp.dma_start(decay[d][:, :, col:col + n], src).then_inc(decay_in[d], 16)

            x2_blk = x2_d.rearrange("(n j p) c -> p n j c", p=P, j=BT)

            def load_x2(n):
                sp.dma_start(x2t, x2_blk[:, bass.ds(n, 1), :, :].rearrange("p o j c -> p (o j) c")).then_inc(x2_in, 16)

            def load_w(b, j):
                sp.dma_start(w_stage[:, j, :], wall_d[:, bass.ds(b * (2 * WSTEP) + j * WSTEP, WSTEP)]).then_inc(w_in[j], 16)

            load_x(0, 0)
            load_x(1, 1)
            sp.wait_ge(decT_copied, 1)
            for r in range(2 * NHD):
                sp.dma_start(decay_d[r, :].rearrange("(n t) -> n t", t=P),
                             decT[r:P - (2 * NHD - 1) + r:2 * NHD, :]).then_inc(dec_out, 16)
            load_w(0, 0)
            load_w(0, 1)
            sp.wait_ge(dec_out, 16 * 2 * NHD)
            sp.wait_ge(pads_ready, 8)
            load_decay(0, 0)
            load_decay(0, 1)

            def body(b, half, par):
                if isinstance(b, int) and b == B - 1:
                    sp.wait_ge(t_ready, B)
                    sp.wait_ge(x2_out[0], 16)
                    sp.wait_ge(x2_out[1], 16)
                    load_x2(0)
                if not (isinstance(b, int) and b == 0):
                    for j in range(2):
                        sp.wait_ge(wlo_ready, b * 2 + j - 1)
                        load_w(b, j)
                if not last(b, 2):
                    sp.wait_ge(base_half, b * 2 + 2)
                    sp.wait_ge(u_ready, b * 2 + 2)
                    load_x(b + 2, par)
                if not last(b, 1):
                    for d in range(2):
                        sp.wait_ge(l_ready, b * 2 + d + 1)
                        load_decay(b + 1, d)
                if not (isinstance(b, int) and b == 0):
                    store_x2(b - 1, 1 - par)

            def store_x2(b, par):
                sp.wait_ge(x2_ready, b * 2 + 2)
                sp.dma_start(x2_seq[:, bass.ds(b, 1), :, :].rearrange("p o j c -> p (o j) c"), base[par]).then_inc(x2_out[par], 16)

            sequences(sp, body)
            store_x2(15, 1)
            sp.wait_ge(x2_out[0], 16 * (B // 2))
            sp.wait_ge(x2_out[1], 16 * (B // 2))
            sp.sem_inc(out_sent, 16)
            barrier(sp, mamba_over)

            out_blk = out_d.rearrange("c (n t) -> c n t", t=TB)

            def out_body(n, par, more):
                if more:
                    sp.wait_ge(x2T_ready, n + 1)
                    sp.wait_ge(x3_ready, n * BT + BT)
                    load_x2(n + 1)
                sp.wait_ge(ob_ready, n + 3)
                sp.dma_start(out_blk[:, bass.ds(n, 1), :].rearrange("c o t -> c (o t)"), ob).then_inc(out_sent, 16)

            blocks(sp, out_body)
            sp.wait_ge(out_sent, 16 * NB + 16)

        @block.gpsimd
        def _(pool):
            pool.memset(wnat[:, 0, 6, :], 0.0).then_inc(init_done, 1)
            pool.memset(wnat[:, 1, 6, :], 0.0).then_inc(init_done, 1)
            pool.memset(half_neg[:, :], -0.5).then_inc(init_done, 1)
            pool.memset(ones[:, :], 1.0).then_inc(init_done, 1)
            pool.memset(eps_t[:, :], EPS).then_inc(init_done, 1)
            for par in range(2):
                pool.memset(stack[par][0][:, 0:3], 0.0).then_inc(pads_ready, 1)
                pool.memset(stack[par][1][:, L - 1:L + 2], 0.0).then_inc(pads_ready, 1)
            pool.wait_ge(init_done, 5)
            for n in range(NB):
                pool.wait_ge(mv_ready, n * BT + BT)
                tokens = x_block(n)
                pool.tensor_tensor(tokens, tokens, bc(mv[:, n * BT:n * BT + BT, 0], 2, C), ALU.subtract).then_inc(centered, 1)
            pool.wait_ge(dt_ready, NB)
            for d, (c0, c1_) in enumerate(((0, L), (P - 1, LB - 1))):
                pool.memset(decay[d][:, :, c0:c0 + 1], 0.0).then_inc(pads_ready, 1)
                pool.memset(decay[d][:, :, c1_:c1_ + 1], 0.0).then_inc(pads_ready, 1)

            def y2(b, d):
                pool.wait_ge(y1_ready, b * 2 + d + 1)
                pool.tensor_tensor(yT[d], yT[d], szT[d], ALU.mult).then_inc(y2_ready, 1)

            def rms_factor(b):
                pool.wait_ge(msq_ready, b + 1)
                pool.tensor_tensor(rms, rms, half_neg[:, 0:2 * JT], ALU.pow).then_inc(rms_ready, 1)

            def rstd2(n):
                pool.wait_ge(mv2_ready, n * BT + BT)
                pool.tensor_tensor(rs2[:, 0, :], mv2[:, :, 1], eps_t[:, :], ALU.add).then_inc(rs2_half, 1)
                pool.wait_ge(rs2_half, n + 1)
                pool.tensor_tensor(rs2[:, 1, :], rs2[:, 0, :], half_neg[:, 0:BT], ALU.pow).then_inc(rs2_ready, 1)

            def low_part(b, j):
                pool.wait_ge(whi_ready, b * 2 + j + 1)
                at = bass.ds(b * (2 * WSTEP) + j * WSTEP, WSTEP)
                pool.tensor_tensor(w_lo[:, at], w_stage[:, j, :], w_hi[:, at].bitcast(F32), ALU.subtract).then_inc(wlo_ready, 1)

            def body(b, half, par):
                start = isinstance(b, int) and b == 0
                if not start:
                    y2(b - 1, 1)
                pool.wait_ge(base_half, b * 2 + 2)
                pool.tensor_tensor(base[par], base[par], bc(rows[:, ROW_OPB:ROW_OPB + C], 1, JT), ALU.add).then_inc(base_ready, 1)
                if isinstance(b, int) and b == B - 1:
                    rstd2(0)
                low_part(b, 0)
                if not start:
                    rms_factor(b - 1)
                low_part(b, 1)
                y2(b, 0)

            sequences(pool, body)
            y2(15, 1)
            rms_factor(15)
            pool.sem_inc(lop_ready, 2)
            pool.wait_ge(rms_ready, B)
            barrier(pool, mamba_over)

            def hidden(q, c):
                pool.wait_ge(a_ready, q + 1)
                pool.wait_ge(s_ready, q + 1)
                pool.wait_ge(lop_ready, q + 1)
                pool.tensor_tensor(h_t[c % 2][:, 0:HS], a_t[c % 2][:, 0:HS], s_t[c % 2][:, 0:HS], ALU.mult).then_inc(hp_ready, 1)

            hidden(0, 0)

            def blk(n, par, more):
                for c in range(NC):
                    q = n * NC + c
                    if more and c == 8:
                        rstd2(n + 1)
                    if more or c + 1 < NC:
                        hidden(q + 1, c + 1)
                    pool.wait_ge(hhi_ready, q + 1)
                    pool.tensor_tensor(h_lo[c % 2][:, 0:HS], h_t[c % 2][:, 0:HS], h_hi[c % 2][:, 0:HS].bitcast(F32), ALU.subtract).then_inc(lop_ready, 1)

            blocks(pool, blk)

        @block.scalar
        def _(act):
            act.wait_ge(inw_in, 32)
            act.wait_ge(init_done, 2)
            for g in range(3):
                for pair in range(2):
                    for s in range(2):
                        k = CW[1] + KCONV * g + TAPS[1][pair][s]
                        act.activation(wnat[:, 1, 2 * g + pair, HALF * s:HALF * s + HALF], inw[:, 1, 1 + g, :],
                                       ACT.Copy, scale=cols[:, k:k + 1])
            act.activation(wnat[:, 1, 6, HALF:P], inw[:, 1, 0, :], ACT.Copy).then_inc(wnat1_ready, 1)
            for i in range(4):
                act.wait_ge(wT_ready, i + 1)
                lo, hi = 4 * i, min(4 * i + 4, 14)
                for m in range(lo, hi):
                    d, s = m // 7, m % 7
                    ins = act.activation(wproj[:, d, s, :], bank[i][:, (m - lo) * P:(m - lo + 1) * P],
                                         ACT.Copy, scale=cols[:, NWS[d]:NWS[d] + 1])
                ins.then_inc(wT_copied, 1)
            for n in range(NB):
                act.wait_ge(xproT_ready, n + 1)
                if n >= 2:
                    act.wait_ge(dt_ready, n - 1)
                act.activation(xT_pro[:, n % 2, :], bank[4 + n % 2][:, :], ACT.Copy).then_inc(xproT_copied, 1)
                if n == NB - 2:
                    act.wait_ge(variance_ready, 1)
                    act.activation(root, variance, ACT.Sqrt).then_inc(root_ready, 1)
            act.wait_ge(params_in, 16 * 4)
            act.activation(ea, rows[:, ROW_ALOG:ROW_ALOG + 2 * NHD], ACT.Exp).then_inc(ea_ready, 1)
            act.activation(gw_hi[:, :], gwt, ACT.Copy).then_inc(gw_ready, 1)
            act.wait_ge(mo_ready, 1)
            for d in range(2):
                ins = act.activation(mo_w[:, d, :], bank[7][:, d * P:d * P + P], ACT.Copy,
                                     scale=cols[:, GN[d]:GN[d] + 1])
            ins.then_inc(mo_copied, 1)
            act.wait_ge(abs_ready, 1)
            act.activation(sp_e, sp_abs, ACT.Exp, scale=-1.0).then_inc(e_ready, 1)
            act.wait_ge(pads_ready, 4)

            def stacks(b, par):
                act.wait_ge(t_ready, b + 1)
                f, r = stack[par]
                T0, T1 = bank[4][:, 0:L], bank[4][:, L:2 * L]
                act.activation(f[0:HALF, 2:2 + L], T0[0:HALF, :], ACT.Copy).then_inc(stack_ready, 1)
                act.activation(f[HALF:P, 3:3 + L], T0[HALF:P, :], ACT.Copy).then_inc(stack_ready, 1)
                act.activation(r[HALF:P, 0:L], T1[HALF:P, :], ACT.Copy).then_inc(stack_ready, 1)
                act.activation(r[0:HALF, 0:L - 1], T1[0:HALF, 1:L], ACT.Copy).then_inc(stack_ready, 1)

            def silus(b, d):
                start = isinstance(b, int) and b == 0
                if not start:
                    act.wait_ge(y1_ready, b * 2 + d - 1)
                    act.wait_ge(xtok_ready, b * 2 + d - 1)
                    act.wait_ge(g_ready, b * 2 + d - 1)
                    act.wait_ge(y2_ready, b * 2 + d - 1)
                act.wait_ge(proj_ready, b * 4 + 2 * d + 1)
                bias = cols[:, CB[d]:CB[d] + 3]
                p0, p1 = bank[2 * d], bank[2 * d + 1]
                act.activation(xT[d], p0[:, 0:L], ACT.Silu, bias=bias[:, 0:1]).then_inc(silu_ready, 1)
                act.activation(bT[d], p0[:, L:2 * L], ACT.Silu, bias=bias[:, 1:2]).then_inc(silu_ready, 1)
                act.wait_ge(proj_ready, b * 4 + 2 * d + 2)
                act.activation(cT[d], p1[:, 0:L], ACT.Silu, bias=bias[:, 2:3]).then_inc(silu_ready, 1)
                act.activation(szT[d], p1[:, L:2 * L], ACT.Silu).then_inc(silu_ready, 1)

            def squares(b, d):
                act.wait_ge(y2_ready, b * 2 + d + 1)
                if not (isinstance(b, int) and b == 0):
                    act.wait_ge(ssq_ready, b)
                act.activation(ysqT[d], yT[d], ACT.Square).then_inc(ysq_ready, 1)

            def residual(b, half, par):
                if isinstance(b, int) and b == 0:
                    act.wait_ge(norm_ready, 1)
                act.wait_ge(x_in[par], half * 16 + 16)
                if not (isinstance(b, int) and b < 2):
                    act.wait_ge(x2_out[par], half * 16)
                for j in range(JT):
                    act.activation(base[par][:, j, :], xt[par][:, j, :], ACT.Identity, bias=c2[:, bass.ds(b * JT + j, 1)],
                                   scale=c1[:, bass.ds(b * JT + j, 1)]).then_inc(base_half, 1)

            def x3_high(n, par):
                act.wait_ge(x3T_ready, n + 1)
                act.activation(x3_hi[par][:, :], bank[x3_bank(n)][:, :], ACT.Copy).then_inc(x3hi_ready, 1)

            def x2_copy(n, par):
                act.wait_ge(x2T_ready, n + 1)
                if not (isinstance(n, int) and n == 0):
                    act.wait_ge(ob_ready, n + 1)
                act.activation(x2T[par], bank[7][:, :], ACT.Copy).then_inc(x2T_copied, 1)

            def gate_exp(n):
                act.wait_ge(logits_ready, n + 1)
                act.activation(nexp, bank[logit_bank(n)][:, 0:BT * E].rearrange("p (a b) -> p a b", a=BT), ACT.Exp, scale=-1.0).then_inc(nexp_ready, 1)

            def high_part(b, j):
                act.wait_ge(w_in[j], b * 16 + 16)
                act.activation(w_hi[:, bass.ds(b * (2 * WSTEP) + j * WSTEP, WSTEP)], w_stage[:, j, :], ACT.Copy).then_inc(whi_ready, 1)

            stacks(0, 0)
            act.wait_ge(arg_ready, 1)
            act.activation(sp_arg, sp_abs, ACT.Exp, scale=-1.0).then_inc(dec_ready, 1)
            act.wait_ge(decT_ready, 1)
            act.activation(decT, bank[7][:, L:L + P], ACT.Copy).then_inc(decT_copied, 1)

            def body(b, half, par):
                start = isinstance(b, int) and b == 0
                silus(b, 0)
                if not start:
                    squares(b - 1, 0)
                if not last(b, 1):
                    if not start:
                        act.wait_ge(proj_ready, b * 4)
                    stacks(b + 1, 1 - par)
                if not start:
                    squares(b - 1, 1)
                residual(b, half, par)
                high_part(b, 0)
                silus(b, 1)
                if isinstance(b, int) and b == B - 1:
                    x3_high(0, 0)
                high_part(b, 1)

            sequences(act, body)
            squares(15, 0)
            gate_exp(0)
            squares(15, 1)
            def rw_copy(n, par):
                act.wait_ge(rwT_ready, n + 1)
                act.activation(rwb[par], bank[7][:, :], ACT.Copy).then_inc(rwb_ready, 1)

            def silu(q, c):
                act.wait_ge(gate_ready, q + 1)
                act.activation(s_t[c % 2], bank[c % 2][:, :], ACT.Silu).then_inc(s_ready, 1)

            x2_copy(0, 0)
            silu(0, 0)
            rw_copy(0, 0)
            act.wait_ge(rwb_ready, 1)
            barrier(act, mamba_over)

            def blk(n, par, more):
                for c in range(NC):
                    q = n * NC + c
                    if more:
                        if c == 14:
                            x3_high(n + 1, 1 - par)
                        if c == 15:
                            x2_copy(n + 1, 1 - par)
                        if c == 20:
                            gate_exp(n + 1)
                        if c == 41:
                            rw_copy(n + 1, 1 - par)
                    if more or c + 1 < NC:
                        silu(q + 1, c + 1)
                    act.wait_ge(hp_ready, q + 1)
                    act.wait_ge(hv_ready, q + 1)
                    act.wait_ge(down_done, q + 1)
                    act.activation(h_hi[c % 2][:, :], h_t[c % 2], ACT.Copy).then_inc(hhi_ready, 1)

            blocks(act, blk)

        @block.vector
        def _(dve):
            links = [0]

            def link(ins):
                links[0] += 1
                ins.then_inc(link_v, 1)
                dve.wait_ge(link_v, links[0])

            factors = mean_rms.rearrange("p n k -> p (n k)")

            def normed(b, half, par):
                dve.wait_ge(x_in[par], half * 16 + 16)
                for j in range(JT):
                    src = bc(xt[par][:, j, :].rearrange("p (d c) -> p d c", d=2), 2, 2)
                    i = b * JT + j
                    dve.tensor_scalar(u2[:, j, :].rearrange("p (d r c) -> p d r c", d=2, r=2), src,
                                      factors[:, bass.ds(i * 2, 1)], factors[:, bass.ds(i * 2 + 1, 1)],
                                      ALU.subtract, ALU.mult).then_inc(u_ready, 1)

            dve.wait_ge(inw_in, 32)
            dve.wait_ge(init_done, 1)
            for g in range(3):
                for pair in range(2):
                    for s in range(2):
                        k = CW[0] + KCONV * g + TAPS[0][pair][s]
                        dve.tensor_scalar(wnat[:, 0, 2 * g + pair, HALF * s:HALF * s + HALF],
                                          inw[:, 0, 1 + g, :], cols[:, k:k + 1], None, ALU.mult)
            dve.tensor_copy(wnat[:, 0, 6, 0:HALF], inw[:, 0, 0, :]).then_inc(wnat_ready, 1)
            dve.tensor_scalar(wdt, cols[:, WDT:WDT + 2 * NHD], cols[:, NWN:NWN + 1], None, ALU.mult).then_inc(wdt_ready, 1)
            for n in range(NB + 1):
                if n < NB:
                    dve.wait_ge(x_all_in[n], 16)
                    for i in range(n * BT, n * BT + BT):
                        dve.bn_stats(stats[:, i, :], x_block(n)[:, i - n * BT, :]).then_inc(stats_ready, 1)
                if n > 0:
                    dve.wait_ge(stats_ready, n * BT)
                    for i in range(n * BT - BT, n * BT):
                        dve.bn_aggr(mv[:, i, :], stats[:, i, :]).then_inc(mv_ready, 1)
            dve.wait_ge(mv_ready, NT)
            mean, var = mv[:, :, 0], mv[:, :, 1]
            link(dve.tensor_scalar(variance[:, 0, :], var, EPS, None, ALU.add))
            dve.scalar_tensor_tensor(variance[:, 1, :], variance[:, 0, :], EPS, var, ALU.mult, ALU.add).then_inc(variance_ready, 1)
            dve.wait_ge(root_ready, 1)
            link(dve.reciprocal(factor, root))
            link(dve.tensor_tensor(newton, factor, factor, ALU.mult))
            link(dve.tensor_tensor(newton, newton, variance, ALU.mult))
            link(dve.tensor_scalar(newton, newton, -0.5, 1.5, ALU.mult, ALU.add))
            link(dve.tensor_tensor(factor, factor, newton, ALU.mult))
            dve.wait_ge(params_in, 16 * 4)
            dve.wait_ge(dt_ready, NB)
            nt_h = "p (n h) -> p n h"
            dtb = bc(rows[:, ROW_DTB:ROW_DTB + 2 * NHD], 1, NT)
            v3 = sp_arg.rearrange(nt_h, n=NT)
            link(dve.tensor_tensor(v3, bank[6][:, 0:P].rearrange(nt_h, n=NT), bc(factor[:, 1, :], 2, 2 * NHD), ALU.mult))
            link(dve.tensor_tensor(v3, v3, dtb, ALU.add))
            dve.scalar_tensor_tensor(sp_abs, sp_arg, -1.0, sp_arg, ALU.mult, ALU.max).then_inc(abs_ready, 1)
            dve.tensor_copy(mean_rms[:, :, 0], mean)
            link(dve.tensor_copy(mean_rms[:, :, 1], factor[:, 1, :]))
            normed(0, 0, 0)
            dve.wait_ge(e_ready, 1)
            link(dve.tensor_scalar(sp_s2, sp_e, 2.0, None, ALU.add))
            link(dve.reciprocal(sp_p, sp_s2))
            link(dve.tensor_tensor(sp_s, sp_e, sp_p, ALU.mult))
            link(dve.tensor_tensor(sp_s2, sp_s, sp_s, ALU.mult))
            link(dve.tensor_scalar(sp_p, sp_s2, 1.0 / 15, None, ALU.mult))
            for k in (13, 11, 9, 7, 5, 3):
                link(dve.scalar_tensor_tensor(sp_p, sp_p, 1.0 / k, sp_s2, ALU.add, ALU.mult))
            link(dve.scalar_tensor_tensor(sp_p, sp_p, 1.0, sp_s, ALU.add, ALU.mult))
            link(dve.tensor_scalar(sp_s, sp_arg, 0.0, None, ALU.max))
            dt_flat = dt_all.rearrange("p n h -> p (n h)")
            link(dve.scalar_tensor_tensor(dt_flat, sp_p, 2.0, sp_s, ALU.mult, ALU.add))
            dve.wait_ge(ea_ready, 1)
            dve.tensor_tensor(sp_abs.rearrange(nt_h, n=NT), dt_all, bc(ea, 1, NT), ALU.mult).then_inc(arg_ready, 1)
            link(dve.tensor_scalar(c1, factor[:, 0, :], 1.0, None, ALU.add))
            dve.scalar_tensor_tensor(c2, mean, -1.0, factor[:, 0, :], ALU.mult, ALU.mult).then_inc(norm_ready, 1)
            dve.wait_ge(gw_ready, 1)
            dve.tensor_tensor(gw_lo[:, :], gwt, gw_hi[:, :].bitcast(F32), ALU.subtract).then_inc(gw_ready, 1)

            def scan(b, d):
                if not (isinstance(b, int) and b == 0):
                    dve.wait_ge(y_ready, b * 2 + d - 1)
                else:
                    dve.wait_ge(pads_ready, 8)
                dve.wait_ge(decay_in[d], b * 32 + 32)
                way = slice(None, None, 1 if d == 0 else -1)
                for h in range(NHD):
                    ins = dve.tensor_tensor_scan(lmask[d][:, h, way], decay[d][:, h, way], scan_eye[:, way],
                                                 0.0, ALU.mult, ALU.add)
                ins.then_inc(l_ready, 1)

            def xdt_step(b, d):
                dve.wait_ge(xtok_ready, b * 2 + d + 1)
                if not (isinstance(b, int) and b == 0):
                    dve.wait_ge(y_ready, b * 2 + d - 1)
                dtv = dt_all.rearrange("p (b j) h -> p b j h", j=JT)[:, bass.ds(b, 1), :, NHD * d:NHD * d + NHD]
                dtv = dtv.rearrange("p o j h -> p (o j) h")
                dve.tensor_tensor(xdt[d], bank[5][:, 0:L].rearrange("p (j h c) -> p j h c", j=JT, h=NHD),
                                  bc(dtv, 3, HD), ALU.mult).then_inc(xdt_ready, 1)

            def m_step(b, d):
                dve.wait_ge(g_ready, b * 2 + d + 1)
                dve.wait_ge(l_ready, b * 2 + d + 1)
                dve.tensor_tensor(lmask[d], bc(bank[6][:, 0:LB], 1, NHD), lmask[d], ALU.mult).then_inc(m_ready, 1)

            def y1(b, d):
                dve.wait_ge(y_ready, b * 2 + d + 1)
                dve.wait_ge(silu_ready, b * 8 + 4 * d + 1)
                if not (isinstance(b, int) and b == 0):
                    dve.wait_ge(out_ready, b)
                    dve.wait_ge(ysq_ready, b * 2)
                dve.scalar_tensor_tensor(yT[d], xT[d], cols[:, DCOL[d]:DCOL[d] + 1], bank[7][:, 0:L],
                                         ALU.mult, ALU.add).then_inc(y1_ready, 1)

            def mean_square(b):
                dve.wait_ge(ssq_ready, b + 1)
                dve.wait_ge(x2_ready, b * 2)
                dve.tensor_scalar(rms, bank[7][:, L:L + 2 * JT], 1.0 / C, EPS, ALU.mult, ALU.add).then_inc(msq_ready, 1)

            def x2_step(b, par):
                dve.wait_ge(out_ready, b + 1)
                dve.wait_ge(rms_ready, b + 1)
                dve.wait_ge(base_ready, b + 1)
                for d in range(2):
                    for j in range(JT):
                        m = d * JT + j
                        dve.scalar_tensor_tensor(base[par][:, j, :], bank[4][:, m * P:m * P + P], rms[:, m:m + 1],
                                                 base[par][:, j, :], ALU.mult, ALU.add)\
                           .then_inc(x2_half if d == 0 else x2_ready, 1)
                    if d == 0:
                        dve.wait_ge(x2_half, b * 2 + 2)

            ROUTE = 31
            g8 = "p t (g e) -> p (t g) e"

            def route(n, piece):
                r = n * ROUTE

                def rlink(k, ins):
                    ins.then_inc(route_link, 1)
                    dve.wait_ge(route_link, r + k)

                ch = choice.rearrange(g8, g=NG)
                if piece == 0:
                    dve.wait_ge(nexp_ready, n + 1)
                    rlink(1, dve.tensor_scalar(choice, nexp, 1.0, None, ALU.add))
                    rlink(2, dve.reciprocal(scores, choice))
                    rlink(3, dve.tensor_tensor(choice, scores, bc(rows[:, ROW_GB:ROW_GB + E], 1, BT), ALU.add))
                elif piece == 1:
                    rlink(4, dve.tensor_tensor(t1h, ch[:, :, 0:4], ch[:, :, 4:8], ALU.max))
                    rlink(5, dve.tensor_tensor(t1l, ch[:, :, 0:4], ch[:, :, 4:8], ALU.min))
                    rlink(6, dve.tensor_tensor(t2h, t1h[:, :, 0:2], t1h[:, :, 2:4], ALU.max))
                    rlink(7, dve.tensor_tensor(t2a, t1h[:, :, 0:2], t1h[:, :, 2:4], ALU.min))
                elif piece == 2:
                    rlink(8, dve.tensor_tensor(t2b, t1l[:, :, 0:2], t1l[:, :, 2:4], ALU.max))
                    rlink(9, dve.tensor_tensor(t2l, t2a, t2b, ALU.max))
                    rlink(10, dve.tensor_tensor(t3h, t2h[:, :, 0:1], t2h[:, :, 1:2], ALU.max))
                    rlink(11, dve.tensor_tensor(t3a, t2h[:, :, 0:1], t2h[:, :, 1:2], ALU.min))
                elif piece == 3:
                    rlink(12, dve.tensor_tensor(t3b, t2l[:, :, 0:1], t2l[:, :, 1:2], ALU.max))
                    rlink(13, dve.tensor_tensor(t3b, t3a, t3b, ALU.max))
                    rlink(14, dve.tensor_tensor(gs, t3h, t3b, ALU.add))
                elif piece == 4:
                    gsv = gs.rearrange("p (t g) o -> p t (g o)", t=BT)
                    other, own = bc(gsv, 2, NG), bc(gsv, 3, NG)
                    v1 = cmp1.rearrange("p t (g o) -> p t g o", g=NG)
                    v2 = cmp2.rearrange("p t (g o) -> p t g o", g=NG)
                    rlink(15, dve.tensor_tensor(v1, other, own, ALU.is_gt))
                    rlink(16, dve.tensor_tensor(v2, other, own, ALU.is_equal))
                elif piece == 5:
                    rlink(17, dve.tensor_tensor(cmp2, cmp2, bc(tri[:, :], 1, BT), ALU.mult))
                    rlink(18, dve.tensor_tensor(cmp1, cmp1, cmp2, ALU.add))
                elif piece == 6:
                    rlink(19, dve.tensor_reduce(rank, cmp1.rearrange("p t (g o) -> p t g o", g=NG), X, ALU.add))
                    rlink(20, dve.tensor_scalar(rank, rank, TOPG - 0.5, None, ALU.is_lt))
                elif piece == 7:
                    gm = bc(rank.rearrange("p t g -> p (t g)"), 2, EPG)
                    rlink(21, dve.tensor_tensor(masked.rearrange(g8, g=NG), ch, gm, ALU.mult))
                elif piece == 8:
                    for t in range(BT):
                        ins = dve.max(m8[:, t, :], masked[:, t, :])
                    rlink(22, ins)
                elif piece == 9:
                    for t in range(BT):
                        ins = dve.match_replace(repl[:, t, :], m8[:, t, :], masked[:, t, :], LOWEST)
                    rlink(23, ins)
                elif piece == 10:
                    rlink(24, dve.tensor_tensor(wsel, repl, masked, ALU.not_equal))
                    rlink(25, dve.tensor_tensor(wsel, wsel, scores, ALU.mult))
                elif piece == 11:
                    rlink(26, dve.tensor_reduce(den, wsel, X, ALU.add))
                    rlink(27, dve.tensor_scalar(den, den, 1e-20, None, ALU.add))
                    rlink(28, dve.reciprocal(den, den))
                elif piece == 12:
                    rlink(29, dve.tensor_scalar(den, den, SCALE, None, ALU.mult))
                    rlink(30, dve.tensor_tensor(wsel, wsel, bc(den, 2, E), ALU.mult))
                elif piece == 13:
                    if not (isinstance(n, int) and n == 0):
                        dve.wait_ge(rwT_ready, n)
                    rlink(31, dve.tensor_copy(rwp[:, :, 0:E], wsel))
                    dve.tensor_copy(rwp[:, :, E:2 * E], wsel).then_inc(rwp_ready, 1)

            def stats2(n, t0, t1):
                if t0 == 0:
                    dve.wait_ge(x2_in, n * 16 + 16)
                for t in range(t0, t1):
                    dve.bn_stats(st2[:, t, :], x2t[:, t, :]).then_inc(stat2_ready, 1)

            def aggr2(n):
                for t in range(BT):
                    dve.bn_aggr(mv2[:, t, :], st2[:, t, :]).then_inc(mv2_ready, 1)

            def x3_step(n, t0, t1):
                if t0 == 0:
                    dve.wait_ge(rs2_ready, n + 1)
                for t in range(t0, t1):
                    dve.tensor_scalar(x3t[:, t, :], x2t[:, t, :], mv2[:, t, 0:1], rs2[:, 1, t:t + 1],
                                      ALU.subtract, ALU.mult).then_inc(x3_ready, 1)

            def x3_low(n, par):
                dve.wait_ge(x3hi_ready, n + 1)
                dve.tensor_tensor(x3_lo[par][:, :], bank[x3_bank(n)][:, :], x3_hi[par][:, :].bitcast(F32), ALU.subtract).then_inc(x3lo_ready, 1)

            dve.wait_ge(t_ready, 1)
            normed(1, 0, 1)

            def body(b, half, par):
                start = isinstance(b, int) and b == 0
                final = isinstance(b, int) and b == B - 1
                scan(b, 0)
                if not start:
                    y1(b - 1, 1)
                scan(b, 1)
                if final:
                    stats2(0, 0, BT)
                xdt_step(b, 0)
                m_step(b, 0)
                if final:
                    dve.wait_ge(stat2_ready, BT)
                    aggr2(0)
                if not start:
                    mean_square(b - 1)
                if final:
                    x3_step(0, 0, BT)
                xdt_step(b, 1)
                m_step(b, 1)
                if final:
                    x3_low(0, 0)
                    y1(b, 0)
                if not start:
                    x2_step(b - 1, 1 - par)
                if not final:
                    y1(b, 0)
                if not last(b, 2):
                    dve.wait_ge(t_ready, b + 2)
                    normed(b + 2, half + 1, par)

            sequences(dve, body)
            y1(15, 1)
            for piece in range(14):
                if piece == 1:
                    mean_square(15)
                if piece == 7:
                    x2_step(15, 1)
                route(0, piece)
            dve.sem_inc(ob_ready, 2)
            dve.sem_inc(lov_ready, 2)
            dve.wait_ge(x2_ready, 2 * B)
            barrier(dve, mamba_over)

            def weigh(n, q, c, par):
                dve.wait_ge(up_ready, q + 1)
                if c % NC < RC:
                    if c % NC == 0:
                        dve.wait_ge(rwb_ready, n + 1)
                    dve.tensor_tensor(a_t[c % 2], bank[2 + c % 2][:, :], rwb[par], ALU.mult).then_inc(a_ready, 1)
                else:
                    dve.tensor_copy(a_t[c % 2], bank[2 + c % 2][:, :]).then_inc(a_ready, 1)

            def hidden(q, c):
                dve.wait_ge(a_ready, q + 1)
                dve.wait_ge(s_ready, q + 1)
                dve.wait_ge(lov_ready, q + 1)
                dve.tensor_tensor(h_t[c % 2][:, HS:TB], a_t[c % 2][:, HS:TB], s_t[c % 2][:, HS:TB], ALU.mult).then_inc(hv_ready, 1)

            weigh(0, 0, 0, 0)
            weigh(0, 1, 1, 0)
            hidden(0, 0)

            def step(n, c, par, more):
                q = n * NC + c
                if more:
                    if c in (5, 6):
                        stats2(n + 1, 2 * (c - 5), 2 * (c - 5) + 2)
                    if c == 7:
                        dve.wait_ge(stat2_ready, n * BT + 2 * BT)
                    if c in (10, 11):
                        x3_step(n + 1, 2 * (c - 10), 2 * (c - 10) + 2)
                    if c == 16:
                        x3_low(n + 1, 1 - par)
                    if 22 <= c < 36:
                        route(n + 1, c - 22)
                if more or c + 1 < NC:
                    hidden(q + 1, c + 1)
                if more and c == 7:
                    aggr2(n + 1)
                dve.wait_ge(hhi_ready, q + 1)
                dve.tensor_tensor(h_lo[c % 2][:, HS:TB], h_t[c % 2][:, HS:TB], h_hi[c % 2][:, HS:TB].bitcast(F32), ALU.subtract).then_inc(lov_ready, 1)
                if more or c + 2 < NC:
                    dve.wait_ge(hp_ready, q + 1)
                    if c + 2 < NC:
                        weigh(n, q + 2, c + 2, par)
                    else:
                        weigh(n + 1, q + 2, c + 2, 1 - par)

            for c in range(LAG):
                step(0, c, 0, True)

            def blk(n, par, more):
                for c in range(LAG, NC + LAG if more else NC):
                    step(n, c, par, more)
                dve.wait_ge(down_done, n * NC + NC + 2)
                dve.wait_ge(x2T_copied, n + 1)
                dve.wait_ge(out_sent, n * 16 + 16)
                dve.tensor_tensor(ob, bank[4 + par][:, :], x2T[par], ALU.add).then_inc(ob_ready, 1)

            blocks(dve, blk)

        @block.tensor
        def _(pe):
            pe.wait_ge(eye_in, 16)
            for i in range(4):
                lo, hi = 4 * i, min(4 * i + 4, 14)
                pe.wait_ge(wnat_ready, 1)
                if hi > 7:
                    pe.wait_ge(wnat1_ready, 1)
                for m in range(lo, hi):
                    ins = pe.transpose(bank[i][:, (m - lo) * P:(m - lo + 1) * P], wnat[:, m // 7, m % 7, :], ident)
                ins.then_inc(wT_ready, 1)
            pe.wait_ge(wdt_ready, 1)
            for n in range(NB + 1):
                if n < NB:
                    pe.wait_ge(centered, n + 1)
                    if n >= 2:
                        pe.wait_ge(xproT_copied, n - 1)
                    for j in range(BT):
                        ins = pe.transpose(bank[4 + n % 2][:, j * P:j * P + P], x_block(n)[:, j, :], ident)
                    ins.then_inc(xproT_ready, 1)
                if n > 0:
                    pe.wait_ge(xproT_copied, n)
                    for j in range(BT):
                        i = ((n - 1) * BT + j) * 2 * NHD
                        ins = pe.matmul(bank[6][:, i:i + 2 * NHD], xT_pro[:, (n - 1) % 2, j * P:j * P + P], wdt, start=True, stop=True)
                    ins.then_inc(dt_ready, 1)
            pe.wait_ge(params_in, 16 * 4)
            for d in range(2):
                ins = pe.matmul(bank[7][:, d * P:d * P + P], mo_sb[0:HALF, 2 * d, :], mo_sb[0:HALF, 2 * d + 1, :], start=True, stop=True)
            ins.then_inc(mo_ready, 1)

            def decays_turned():
                pe.wait_ge(dec_ready, 1)
                pe.transpose(bank[7][:, L:L + P], sp_arg, ident).then_inc(decT_ready, 1)

            def tokensT(b):
                pe.wait_ge(u_ready, b * 2 + 2)
                for d in range(2):
                    for j in range(JT):
                        ins = pe.transpose(bank[4][:, d * L + j * P:d * L + j * P + P],
                                           u2[:, j, d * C:d * C + C], ident)
                ins.then_inc(t_ready, 1)

            def proj(b, d, par):
                pe.wait_ge(stack_ready, b * 4 + 4)
                if not (isinstance(b, int) and b == 0):
                    pe.wait_ge(silu_ready, b * 8 + 4 * d - 4)
                elif d == 0:
                    pe.wait_ge(wT_copied, 4)
                s = stack[par][d]
                near, far = (s[:, 2:2 + L], s[:, 0:L]) if d == 0 else (s[:, 0:L], s[:, 2:2 + L])
                for half in range(2):
                    if half == 1 and d == 0 and isinstance(b, int) and b == 0:
                        decays_turned()
                    for g in range(2):
                        w = 2 * half + g
                        o = bank[2 * d + half][:, g * L:g * L + L]
                        if w < 3:
                            pe.matmul(o, wproj[:, d, 2 * w, :], near, start=True, stop=False)
                            ins = pe.matmul(o, wproj[:, d, 2 * w + 1, :], far, start=False, stop=True)
                        else:
                            ins = pe.matmul(o, wproj[:, d, 6, :], near, start=True, stop=True)
                    ins.then_inc(proj_ready, 1)

            def scores_of(b, d):
                pe.wait_ge(silu_ready, b * 8 + 4 * d + 3)
                if d or not (isinstance(b, int) and b == 0):
                    pe.wait_ge(m_ready, b * 2 + d)
                    pe.wait_ge(xdt_ready, b * 2 + d)
                G = bank[6]
                for j in range(JT):
                    ins = pe.transpose(bank[5][:, j * P:j * P + P], xT[d][:, j * P:j * P + P], ident)
                ins.then_inc(xtok_ready, 1)
                if d == 0:
                    pe.matmul(G[:, 0:L], bT[d][:, 0:P], cT[d][:, 0:L], start=True, stop=True)
                    ins = pe.matmul(G[:, L:LB], bT[d][:, P:L], cT[d][:, P:L], start=True, stop=True)
                else:
                    pe.matmul(G[:, 0:P], bT[d][:, 0:P], cT[d][:, 0:P], start=True, stop=True)
                    ins = pe.matmul(G[:, P:LB], bT[d][:, P:L], cT[d][:, 0:L], start=True, stop=True)
                ins.then_inc(g_ready, 1)

            def y_of(b, d):
                pe.wait_ge(m_ready, b * 2 + d + 1)
                pe.wait_ge(xdt_ready, b * 2 + d + 1)
                if d or not (isinstance(b, int) and b == 0):
                    pe.wait_ge(y1_ready, b * 2 + d)
                if not (isinstance(b, int) and b == 0):
                    pe.wait_ge(msq_ready, b)
                for h in range(NHD):
                    o = bank[7][HD * h:HD * h + HD, :]
                    m = lmask[d][:, h, :]
                    src, one, both = (0, 0, P) if d == 0 else (1, P, 0)
                    m0 = m[:, 0:L] if d == 0 else m[:, P:LB]
                    m1 = m[:, L:LB] if d == 0 else m[:, 0:P]
                    pe.matmul(o[:, one:one + P], xdt[d][:, src, h, :], m0[:, one:one + P], start=True, stop=True)
                    pe.matmul(o[:, both:both + P], xdt[d][:, src, h, :], m0[:, both:both + P], start=True, stop=False)
                    ins = pe.matmul(o[:, both:both + P], xdt[d][:, 1 - src, h, :], m1, start=False, stop=True)
                ins.then_inc(y_ready, 1)

            def out_of(b):
                pe.wait_ge(y2_ready, b * 2 + 2)
                pe.wait_ge(ysq_ready, b * 2 + 2)
                for d in range(2):
                    for j in range(JT):
                        m = d * JT + j
                        ins = pe.matmul(bank[7][:, L + m:L + m + 1], ysqT[d][:, j * P:j * P + P], ones[:, :], start=True, stop=True)
                ins.then_inc(ssq_ready, 1)
                if not (isinstance(b, int) and b == 0):
                    pe.wait_ge(x2_ready, b * 2)
                if not last(b, 2):
                    pe.wait_ge(stack_ready, b * 4 + 12)
                for d in range(2):
                    for j in range(JT):
                        m = d * JT + j
                        ins = pe.matmul(bank[4][:, m * P:m * P + P], yT[d][:, j * P:j * P + P], mo_w[:, d, :], start=True, stop=True)
                ins.then_inc(out_ready, 1)

            tokensT(0)

            def turn_x2(n):
                pe.wait_ge(x2_in, n * 16 + 16)
                if not (isinstance(n, int) and n == 0):
                    pe.wait_ge(rwb_ready, n)
                for t in range(BT):
                    ins = pe.transpose(bank[7][:, t * P:t * P + P], x2t[:, t, :], ident)
                ins.then_inc(x2T_ready, 1)

            def turn_x3(n):
                pe.wait_ge(x3_ready, n * BT + BT)
                if not (isinstance(n, int) and n == 0):
                    pe.wait_ge(nexp_ready, n)
                for t in range(BT):
                    ins = pe.transpose(bank[x3_bank(n)][:, t * P:t * P + P], x3t[:, t, :], ident)
                ins.then_inc(x3T_ready, 1)

            def logits(n, par):
                pe.wait_ge(x3lo_ready, n + 1)
                pe.wait_ge(gw_ready, 2)
                for t in range(BT):
                    o = bank[logit_bank(n)][:, t * E:t * E + E]
                    hi, lo = x3_hi[par][:, t * P:t * P + P], x3_lo[par][:, t * P:t * P + P]
                    pe.matmul(o, hi, gw_hi[:, :], start=True, stop=False)
                    pe.matmul(o, lo, gw_hi[:, :], start=False, stop=False)
                    ins = pe.matmul(o, hi, gw_lo[:, :], start=False, stop=True)
                ins.then_inc(logits_ready, 1)

            def body(b, half, par):
                start = isinstance(b, int) and b == 0
                proj(b, 0, par)
                if not last(b, 1):
                    if not start:
                        pe.wait_ge(x2_ready, b * 2 - 2)
                    pe.wait_ge(stack_ready, b * 4 + 4)
                    tokensT(b + 1)
                if not start:
                    y_of(b - 1, 1)
                proj(b, 1, par)
                scores_of(b, 0)
                if not start:
                    out_of(b - 1)
                if isinstance(b, int) and b == B - 1:
                    pe.wait_ge(silu_ready, b * 8 + 4)
                    turn_x3(0)
                scores_of(b, 1)
                y_of(b, 0)

            sequences(pe, body)
            logits(0, 0)
            y_of(15, 1)
            out_of(15)
            pe.wait_ge(msq_ready, B)
            turn_x2(0)
            def w(kind, c):
                at = (kind * NC + c) * P
                return w_hi[:, at:at + P], w_lo[:, at:at + P]

            def three(o, wk, hi, lo, first, final):
                pe.matmul(o, wk[0], hi, start=first, stop=False)
                pe.matmul(o, wk[1], hi, start=False, stop=False)
                return pe.matmul(o, wk[0], lo, start=False, stop=final)

            def turn_rw(n):
                pe.wait_ge(rwp_ready, n + 1)
                pe.wait_ge(x2T_copied, n + 1)
                for t in range(BT):
                    ins = pe.transpose(bank[7][:, t * P:t * P + P], rwp[:, t, :], ident)
                ins.then_inc(rwT_ready, 1)

            def gate_up(c, odd, par):
                hi, lo = x3_hi[par][:, :], x3_lo[par][:, :]
                three(bank[2 + odd][:, :], w(1, c), hi, lo, True, True).then_inc(up_ready, 1)
                three(bank[odd][:, :], w(0, c), hi, lo, True, True).then_inc(gate_ready, 1)

            pe.wait_ge(whi_ready, 2 * B)
            pe.wait_ge(wlo_ready, 2 * B)
            pe.wait_ge(silu_ready, 8 * B)
            pe.wait_ge(nexp_ready, 1)
            gate_up(0, 0, 0)
            gate_up(1, 1, 0)
            turn_rw(0)
            pe.sem_inc(down_done, 2)
            pe.wait_ge(rwT_ready, 1)
            barrier(pe, mamba_over)

            pe.wait_ge(s_ready, 1)
            pe.wait_ge(a_ready, 1)
            gate_up(2, 0, 0)

            def blk(n, par, more):
                for c in range(NC):
                    q = n * NC + c
                    if more:
                        if c == 12:
                            turn_x2(n + 1)
                            turn_x3(n + 1)
                        if c == 18:
                            logits(n + 1, 1 - par)
                        if c == 39:
                            turn_rw(n + 1)
                    if more or c + LAG < NC:
                        pe.wait_ge(s_ready, q + 2)
                        pe.wait_ge(a_ready, q + 2)
                        gate_up((c + LAG) % NC, (c + LAG) % 2, par if c + LAG < NC else 1 - par)
                    if c == 0:
                        pe.wait_ge(ob_ready, n + 1)
                    pe.wait_ge(lop_ready, q + 3)
                    pe.wait_ge(lov_ready, q + 3)
                    three(bank[4 + par][:, :], w(2, c), h_hi[c % 2][:, :], h_lo[c % 2][:, :],
                          c == 0, c == NC - 1).then_inc(down_done, 1)

            blocks(pe, blk)


def kernel(**inputs):
    import numpy as np
    import concourse.bacc as bacc
    from concourse.bass_utils import run_bass_kernel_spmd as run

    a = {k: np.asarray(v) for k, v in inputs.items()}

    def at(name):
        return a["L0_attn_" + name]

    f32 = np.float32
    cols = np.zeros((P, NCOL), f32)
    rows = np.zeros((1, NROW), f32)
    inw = np.zeros((P, 2, 4, HALF), f32)
    mo = np.zeros((HALF, 4, P), f32)
    for d, p in enumerate(("f_", "b_")):
        cols[:, CW[d]:CW[d] + 12] = at(p + "conv_w").reshape(3, P, KCONV).transpose(1, 0, 2).reshape(P, 12)
        cols[:, CB[d]:CB[d] + 3] = at(p + "conv_b").reshape(3, P).T
        own = slice(HALF * d, HALF * d + HALF)
        cols[:HALF, NWS[d]] = at("norm_w")[own]
        cols[HALF:, NWS[d]] = at("norm_w")[own]
        for h in range(NHD):
            cols[HD * h:HD * h + HD, DCOL[d]] = at(p + "D")[h]
        cols[:, GN[d]] = at(p + "gnorm_w")
        cols[own, WDT + NHD * d:WDT + NHD * d + NHD] = at(p + "in_w")[4 * P:, :].T
        inw[:, d] = at(p + "in_w")[:4 * P].reshape(4, P, HALF).transpose(1, 0, 2)
        rows[0, ROW_DTB + NHD * d:ROW_DTB + NHD * d + NHD] = at(p + "dt_bias")
        rows[0, ROW_ALOG + NHD * d:ROW_ALOG + NHD * d + NHD] = at(p + "A_log")
        mo[:, 2 * d] = at(p + "outp_w")
        mo[:, 2 * d + 1] = at("op_w").T[own]
    cols[:, NWN] = at("norm_w")
    rows[0, ROW_OPB:ROW_OPB + C] = at("op_b")
    rows[0, ROW_GB:ROW_GB + E] = a["L0_ffn_gate_bias"]

    wall = np.zeros((P, 3, NC * P), f32)
    for k, (routed, shared) in enumerate((("Wg", "Sg"), ("Wu", "Su"))):
        wall[:, k, :E * I] = a["L0_ffn_" + routed].transpose(2, 1, 0).reshape(C, I * E)
        wall[:, k, E * I:E * I + SI] = a["L0_ffn_" + shared].T
    down = np.zeros((NC * P, C), f32)
    down[:E * I] = a["L0_ffn_Wd"].transpose(2, 0, 1).reshape(I * E, C)
    down[E * I:E * I + SI] = a["L0_ffn_Sd"].T
    wall[:, 2] = down.reshape(NC, P, C).transpose(1, 0, 2).reshape(P, NC * C)

    const = np.zeros((P, NK), f32)
    const[:, K_SCAN:K_SCAN + P] = np.eye(P, dtype=f32)
    const[:, K_SCAN + L:K_SCAN + LB] = np.eye(P, dtype=f32)
    const[:, K_TRI:NK] = np.tril(np.ones((NG, NG), f32), -1).reshape(1, NG * NG)

    arrays = {
        "x": np.ascontiguousarray(at("x")).reshape(T, C),
        "cols": cols, "rows": rows, "inw": inw, "mo": mo,
        "gwt": np.ascontiguousarray(a["L0_ffn_gate_w"].T),
        "wall": wall.reshape(P, WCOLS), "const": const,
    }
    nc = bacc.Bacc("TRN2", target_bir_lowering=False, num_devices=1)
    args = [nc.dram_tensor("in_" + k, v.shape, mybir.dt.from_np(v.dtype), kind="ExternalInput").ap() for k, v in arrays.items()]
    args.append(nc.dram_tensor("out_0", (C, T), F32, kind="ExternalOutput").ap())
    bidirectional_mamba_moe(nc, *args)
    r = run(nc, [{"in_" + k: v for k, v in arrays.items()}], core_ids=[0])
    return np.ascontiguousarray(r.results[0]["out_0"].T).reshape(B, L, C)
```

```python
from contextlib import ExitStack

import concourse.bass as bass
from concourse import mybir

F32 = mybir.dt.float32
F32R = mybir.dt.float32r
ALU = mybir.AluOpType
ACT = mybir.ActivationFunctionType
X = mybir.AxisListType.X

P = 128
B, L, C = 16, 256, 128
T = B * L
HALF = C // 2
JT = L // P
NT = T // P
NHD = 2
HD = 64
LB = L + P
KCONV = 4
E, I, TOPK, NG, TOPG, SCALE = 64, 88, 8, 8, 4, 2.5
EPG = E // NG
SI = 2 * I
RC = E * I // P
SC = -(-SI // P)
NC = RC + SC
TB = 512
NB = T // TB
BT = TB // P
WCOLS = 3 * NC * P
WSTEP = WCOLS // (2 * B)
LAG = 3
HS = 256
PIECES = 24
EPS = 1e-5
TAPS = (((3, 2), (1, 0)), ((2, 3), (0, 1)))
LOWEST = -3.0e38
NCOL = 2 * (3 * KCONV + 3) + 7 + 4
CW, CB = (0, 15), (12, 27)
NWS = (30, 31)
NWN = 32
DCOL = (33, 34)
GN = (35, 36)
WDT = 37
ROW_DTB, ROW_ALOG, ROW_OPB, ROW_GB, NROW = 0, 4, 8, 8 + C, 8 + C + E
K_SCAN, K_TRI, NK = 0, LB, LB + NG * NG


def bidirectional_mamba_moe(nc, x_d, cols_d, rows_d, inw_d, mo_d, gwt_d, wall_d, const_d, out_d):
    decay_d = nc.dram_tensor("decay_scratch", (2 * NHD, T), F32, kind="Internal").ap()
    x2_d = nc.dram_tensor("x2_scratch", (T, C), F32, kind="Internal").ap()

    with ExitStack() as ctx:
        def sb(name, shape, dt=F32):
            return ctx.enter_context(nc.sbuf_tensor(name, shape, dt))

        def sem(name):
            return ctx.enter_context(nc.semaphore(name))

        w_hi = sb("w_hi", [P, WCOLS], F32R)
        w_lo = sb("w_lo", [P, WCOLS], F32R)
        w_stage = sb("w_stage", [P, 2, WSTEP])
        x3_hi = [sb(f"x3_hi{i}", [P, TB], F32R) for i in range(2)]
        x3_lo = [sb(f"x3_lo{i}", [P, TB], F32R) for i in range(2)]
        h_hi = [sb(f"h_hi{i}", [P, TB], F32R) for i in range(2)]
        h_lo = [sb(f"h_lo{i}", [P, TB], F32R) for i in range(2)]
        stack_hi = [[x3_hi[i], h_hi[i]] for i in range(2)]
        stack_lo = [[x3_lo[i], h_lo[i]] for i in range(2)]
        wp_hi, wp_lo = (w[:, WCOLS - 14 * P:WCOLS].rearrange("p (d s c) -> p d s c", d=2, s=7) for w in (w_hi, w_lo))
        gw_hi = sb("gw_hi", [P, E], F32R)
        gw_lo = sb("gw_lo", [P, E], F32R)
        scan_eye = sb("scan_eye", [P, LB])
        ident = scan_eye[:, 0:P]
        tri = sb("tri", [P, NG * NG])
        rows = sb("rows", [P, NROW])
        half_neg = sb("half_neg", [P, NT])
        eps_t = sb("eps_t", [P, BT])
        ones = sb("ones", [P, 1])

        ARENA = 11850
        arena = sb("arena", [P, ARENA])
        used = [0]

        def cut(*shape):
            n = 1
            for s in shape:
                n *= s
            at = used[0]
            used[0] += n
            assert used[0] <= ARENA, used[0]
            v = arena[:, at:at + n]
            if len(shape) == 2:
                return v.rearrange("p (a b) -> p a b", a=shape[0])
            if len(shape) == 3:
                return v.rearrange("p (a b c) -> p a b c", a=shape[0], b=shape[1])
            return v

        cols = cut(NCOL)
        mo_w = cut(2, P)
        dt_all = cut(NT, 2 * NHD)
        c1 = cut(NT)
        c2 = cut(NT)
        mean_rms = cut(NT, 2)
        at_xt = used[0]
        xt = [cut(JT, C) for _ in range(2)]
        base = [cut(JT, C) for _ in range(2)]
        at_u2 = used[0]
        u2 = cut(JT, 2 * C)
        szT1 = cut(L)
        shared = used[0]
        decay = [cut(NHD, LB) for _ in range(2)]
        at_ysqT = used[0]
        ysqT = [cut(L) for _ in range(2)]
        at_lmask = used[0]
        lmask = [cut(NHD, LB) for _ in range(2)]
        szT = [cut(L), szT1]
        at_xT = used[0]
        xT = [cut(L) for _ in range(2)]
        at_bT = used[0]
        bT = [cut(L) for _ in range(2)]
        cT = [cut(L) for _ in range(2)]
        at_xdt = used[0]
        xdt = [cut(JT, NHD, HD) for _ in range(2)]
        yT = [cut(L) for _ in range(2)]
        rms = cut(2 * JT)
        mamba_end = used[0]
        used[0] = shared
        x_ring = cut(4 * BT, C)
        wnat = cut(2, 7, P)
        inw = cut(2, 4, HALF)
        xT_pro = cut(2, TB)
        stats = cut(NT, 6)
        mv = cut(NT, 2)
        variance, root, newton, factor = (cut(2, NT) for _ in range(4))
        mo_sb = cut(4, P)
        gwt = cut(E)
        wdt = cut(2 * NHD)
        ea = cut(2 * NHD)
        sp_arg, sp_abs, sp_e, sp_s, sp_s2, sp_p = (wnat[:, 0, i, :] for i in range(6))
        decT = sp_s

        def x_block(n):
            if n in (4, 5):
                return w_stage[:, n - 4, 0:BT * C].rearrange("p (j c) -> p j c", j=BT)
            at = (n % 6) * BT
            return x_ring[:, at:at + BT, :]

        used[0] = mamba_end
        x2t = cut(BT, C)
        at_x3t = used[0]
        x3t = cut(BT, C)
        at_nexp = used[0]
        nexp = cut(BT, E)
        scores = cut(BT, E)
        choice = cut(BT, E)
        at_masked = used[0]
        masked = cut(BT, E)
        repl = cut(BT, E)
        wsel = cut(BT, E)
        t2h, t2a, t2l = (cut(BT * NG, 2) for _ in range(3))
        at_t2b = used[0]
        t2b = cut(BT * NG, 2)
        t3b, gs = (cut(BT * NG, 1) for _ in range(2))
        rank = cut(BT, NG)
        m8 = cut(BT, 8)
        den = cut(BT)
        st2 = cut(BT, 6)
        mv2 = cut(BT, 2)
        rs2 = cut(2, BT)
        used[0] = at_nexp
        t1h, t1l = cut(BT * NG, 4), cut(BT * NG, 4)
        used[0] = at_t2b
        t3h, t3a = cut(BT * NG, 1), cut(BT * NG, 1)
        used[0] = at_x3t
        cmp1, cmp2 = cut(BT, NG * NG), cut(BT, NG * NG)
        used[0] = at_masked
        rwp = cut(BT, 2 * E)
        used[0] = 0
        rwb0 = cut(TB)
        assert used[0] <= at_xt
        used[0] = at_lmask
        h_t = [cut(TB) for _ in range(2)]
        used[0] = at_u2
        a0 = cut(TB)
        used[0] = shared
        s_t = [cut(TB) for _ in range(2)]
        a_t = [a0, cut(TB)]
        assert used[0] <= at_ysqT
        used[0] = at_ysqT
        rwb = [rwb0, cut(TB)]
        assert used[0] <= at_lmask
        used[0] = at_xT
        x2T0 = cut(TB)
        assert used[0] <= at_bT
        used[0] = at_xdt
        x2T = [x2T0, cut(TB)]
        ob = cut(TB)
        assert used[0] <= mamba_end

        bank = [ctx.enter_context(nc.psum_tensor(f"bank{i}", [P, 512], F32)) for i in range(8)]

        eye_in = sem("eye_in")
        inw_in = sem("inw_in")
        params_in = sem("params_in")
        x_all_in = [sem(f"x_all_in{i}") for i in range(NB)]
        init_done = sem("init_done")
        stats_ready = sem("stats_ready")
        mv_ready = sem("mv_ready")
        centered = sem("centered")
        variance_ready = sem("variance_ready")
        root_ready = sem("root_ready")
        norm_ready = sem("norm_ready")
        link_v = sem("link_v")
        wnat_ready = sem("wnat_ready")
        wnat1_ready = sem("wnat1_ready")
        wT_ready = sem("wT_ready")
        wT_copied = sem("wT_copied")
        mo_ready = sem("mo_ready")
        mo_copied = sem("mo_copied")
        wdt_ready = sem("wdt_ready")
        ea_ready = sem("ea_ready")
        xproT_ready = sem("xproT_ready")
        xproT_copied = sem("xproT_copied")
        dt_ready = sem("dt_ready")
        abs_ready = sem("abs_ready")
        e_ready = sem("e_ready")
        arg_ready = sem("arg_ready")
        dec_ready = sem("dec_ready")
        decT_ready = sem("decT_ready")
        decT_copied = sem("decT_copied")
        dec_out = [sem(f"dec_out{d}") for d in range(2)]
        gw_ready = sem("gw_ready")

        x_in = [sem(f"x_in{i}") for i in range(2)]
        decay_in = [sem(f"decay_in{i}") for i in range(2)]
        wplo_ready = sem("wplo_ready")
        stacklo_ready = sem("stacklo_ready")
        pads_ready = sem("pads_ready")
        u_ready = sem("u_ready")
        t_ready = sem("t_ready")
        stack_ready = sem("stack_ready")
        proj_ready = sem("proj_ready")
        silu_ready = sem("silu_ready")
        xtok_ready = sem("xtok_ready")
        g_ready = sem("g_ready")
        xdt_ready = sem("xdt_ready")
        l_ready = sem("l_ready")
        m_ready = sem("m_ready")
        y_ready = sem("y_ready")
        y1_ready = sem("y1_ready")
        y2_ready = sem("y2_ready")
        ysq_ready = sem("ysq_ready")
        ssq_ready = sem("ssq_ready")
        out_ready = sem("out_ready")
        msq_ready = sem("msq_ready")
        rms_ready = sem("rms_ready")
        base_half = sem("base_half")
        base_ready = sem("base_ready")
        x2_half = sem("x2_half")
        x2_ready = sem("x2_ready")
        x2_out = [sem(f"x2_out{i}") for i in range(2)]
        w_in = [sem(f"w_in{i}") for i in range(2)]
        whi_ready = sem("whi_ready")
        wlo_ready = sem("wlo_ready")
        mamba_over = sem("mamba_over")

        x2_in = sem("x2_in")
        stat2_ready = sem("stat2_ready")
        mv2_ready = sem("mv2_ready")
        rs2_half = sem("rs2_half")
        rs2_ready = sem("rs2_ready")
        x3_ready = sem("x3_ready")
        x3T_ready = sem("x3T_ready")
        x2T_ready = sem("x2T_ready")
        x3hi_ready = sem("x3hi_ready")
        x2T_copied = sem("x2T_copied")
        x3lo_ready = sem("x3lo_ready")
        logits_ready = sem("logits_ready")
        nexp_ready = sem("nexp_ready")
        route_link = sem("route_link")
        rwp_ready = sem("rwp_ready")
        rwT_ready = sem("rwT_ready")
        rwb_ready = sem("rwb_ready")
        up_ready = sem("up_ready")
        gate_ready = sem("gate_ready")
        s_ready = sem("s_ready")
        a_ready = sem("a_ready")
        hp_ready = sem("hp_ready")
        hv_ready = sem("hv_ready")
        hhi_ready = sem("hhi_ready")
        lop_ready = sem("lop_ready")
        lov_ready = sem("lov_ready")
        down_done = sem("down_done")
        ob_ready = sem("ob_ready")
        out_sent = sem("out_sent")

        block = ctx.enter_context(nc.Block())

        def sequences(eng, body):
            body(0, 0, 0)
            body(1, 0, 1)
            with eng.Fori(0, B // 2 - 2) as k:
                body(k * 2 + 2, k + 1, 0)
                body(k * 2 + 3, k + 1, 1)
            body(14, 7, 0)
            body(15, 7, 1)

        def blocks(eng, body):
            with eng.Fori(0, NB // 2 - 1) as k:
                body(k * 2, 0, True)
                body(k * 2 + 1, 1, True)
            body(NB - 2, 0, True)
            body(NB - 1, 1, False)

        def x3_bank(n):
            return 4 if isinstance(n, int) and n == 0 else 6

        def logit_bank(n):
            return 0 if isinstance(n, int) and n == 0 else 6

        def last(b, n):
            return isinstance(b, int) and b >= B - n

        def last_block(n, k):
            return isinstance(n, int) and n >= NB - k

        def barrier(eng, s):
            eng.sem_inc(s, 1)
            eng.wait_ge(s, 5)

        def bc(ap, axis, n):
            v = ap.unsqueeze(axis)
            shape = list(v.shape)
            shape[axis] = n
            return v.to_broadcast(shape)

        @block.sync
        def _(sp):
            sp.dma_start(cols, cols_d).then_inc(inw_in, 16)
            sp.dma_start(inw, inw_d).then_inc(inw_in, 16)
            x_v = x_d.rearrange("(n p) c -> p n c", p=P)
            for n in range(NB):
                if n >= 6:
                    sp.wait_ge(xproT_ready, n - 5)
                sp.dma_start(x_block(n), x_v[:, BT * n:BT * n + BT, :]).then_inc(x_all_in[n], 16)
                if n == 0:
                    sp.dma_start(scan_eye[:, :], const_d[:, K_SCAN:K_SCAN + LB]).then_inc(eye_in, 16)
                if n == 5:
                    sp.dma_start(rows[:, :], rows_d.partition_broadcast(P).rearrange("p a c -> p (a c)")).then_inc(params_in, 16)
                    sp.dma_start(mo_sb[0:HALF, :, :], mo_d).then_inc(params_in, 16)
                    sp.dma_start(gwt, gwt_d).then_inc(params_in, 16)
                    sp.dma_start(tri[:, :], const_d[:, K_TRI:NK]).then_inc(params_in, 16)
            x_seq = x_d.rearrange("(b j p) c -> p b j c", p=P, j=JT)
            x2_seq = x2_d.rearrange("(b j p) c -> p b j c", p=P, j=JT)

            def load_x(b, par):
                sp.dma_start(xt[par], x_seq[:, bass.ds(b, 1), :, :].rearrange("p o j c -> p (o j) c")).then_inc(x_in[par], 16)

            def load_decay(b, d):
                spans = (((1, 1, L - 1), (L + 1, P + 1, P - 1)), ((0, 0, P - 1), (P, 0, L - 1)))[d]
                for col, t, n in spans:
                    src = decay_d[NHD * d:NHD * d + NHD, bass.ds(b * L + t, n)].partition_broadcast(P)
                    sp.dma_start(decay[d][:, :, col:col + n], src).then_inc(decay_in[d], 16)

            x2_blk = x2_d.rearrange("(n j p) c -> p n j c", p=P, j=BT)

            def load_x2(n):
                sp.dma_start(x2t, x2_blk[:, bass.ds(n, 1), :, :].rearrange("p o j c -> p (o j) c")).then_inc(x2_in, 16)

            def load_w(b, j):
                sp.dma_start(w_stage[:, j, :], wall_d[:, bass.ds(b * (2 * WSTEP) + j * WSTEP, WSTEP)]).then_inc(w_in[j], 16)

            load_x(0, 0)
            load_x(1, 1)
            sp.wait_ge(decT_copied, 1)
            for r in range(2 * NHD):
                sp.dma_start(decay_d[r, :].rearrange("(n t) -> n t", t=P),
                             decT[r:P - (2 * NHD - 1) + r:2 * NHD, :]).then_inc(dec_out[r // NHD], 16)
            sp.wait_ge(dec_out[0], 16 * NHD)
            sp.wait_ge(pads_ready, 12)
            load_decay(0, 0)
            sp.wait_ge(dec_out[1], 16 * NHD)
            load_decay(0, 1)
            load_w(0, 0)
            load_w(0, 1)

            def body(b, half, par):
                if isinstance(b, int) and b == B - 2:
                    sp.wait_ge(x2_out[0], 16)
                    sp.wait_ge(x2_out[1], 16)
                    load_x2(0)
                if not (isinstance(b, int) and b == 0):
                    for j in range(2):
                        sp.wait_ge(wlo_ready, b * 2 + j - 1)
                        load_w(b, j)
                if not last(b, 2):
                    sp.wait_ge(base_half, b * 2 + 2)
                    sp.wait_ge(u_ready, b * 2 + 2)
                    load_x(b + 2, par)
                if not last(b, 1):
                    for d in range(2):
                        sp.wait_ge(l_ready, b * 2 + d + 1)
                        load_decay(b + 1, d)
                if not (isinstance(b, int) and b == 0):
                    store_x2(b - 1, 1 - par)

            def store_x2(b, par):
                sp.wait_ge(x2_ready, b * 2 + 2)
                sp.dma_start(x2_seq[:, bass.ds(b, 1), :, :].rearrange("p o j c -> p (o j) c"), base[par]).then_inc(x2_out[par], 16)

            sequences(sp, body)
            store_x2(15, 1)
            sp.sem_inc(out_sent, 16)
            barrier(sp, mamba_over)
            sp.wait_ge(x2_out[0], 16 * (B // 2))
            sp.wait_ge(x2_out[1], 16 * (B // 2))

            out_blk = out_d.rearrange("c (n t) -> c n t", t=TB)

            sp.wait_ge(x2T_ready, 1)
            sp.wait_ge(x3_ready, BT)
            load_x2(1)

            def out_body(n, par, more):
                if not last_block(n, 2):
                    sp.wait_ge(x2T_ready, n + 2)
                    sp.wait_ge(x3_ready, n * BT + 2 * BT)
                    load_x2(n + 2)
                sp.wait_ge(ob_ready, n + 3)
                sp.dma_start(out_blk[:, bass.ds(n, 1), :].rearrange("c o t -> c (o t)"), ob).then_inc(out_sent, 16)

            blocks(sp, out_body)
            sp.wait_ge(out_sent, 16 * NB + 16)

        @block.gpsimd
        def _(pool):
            pool.memset(wnat[:, 0, 6, :], 0.0).then_inc(init_done, 1)
            pool.memset(wnat[:, 1, 6, :], 0.0).then_inc(init_done, 1)
            pool.memset(half_neg[:, :], -0.5).then_inc(init_done, 1)
            pool.memset(ones[:, :], 1.0).then_inc(init_done, 1)
            pool.memset(eps_t[:, :], EPS).then_inc(init_done, 1)
            for par in range(2):
                for part in (stack_hi, stack_lo):
                    pool.memset(part[par][0][:, 0:3].bitcast(mybir.dt.uint32), 0).then_inc(pads_ready, 1)
                    pool.memset(part[par][1][:, L - 1:L + 2].bitcast(mybir.dt.uint32), 0).then_inc(pads_ready, 1)
            pool.wait_ge(init_done, 5)
            for n in range(NB):
                pool.wait_ge(mv_ready, n * BT + BT)
                tokens = x_block(n)
                pool.tensor_tensor(tokens, tokens, bc(mv[:, n * BT:n * BT + BT, 0], 2, C), ALU.subtract).then_inc(centered, 1)
            pool.wait_ge(dt_ready, NB)
            for d, (c0, c1_) in enumerate(((0, L), (P - 1, LB - 1))):
                pool.memset(decay[d][:, :, c0:c0 + 1], 0.0).then_inc(pads_ready, 1)
                pool.memset(decay[d][:, :, c1_:c1_ + 1], 0.0).then_inc(pads_ready, 1)

            def y2(b, d):
                pool.wait_ge(y1_ready, b * 2 + d + 1)
                pool.wait_ge(silu_ready, b * 8 + 4 * d + 4)
                pool.tensor_tensor(yT[d], yT[d], szT[d], ALU.mult).then_inc(y2_ready, 1)

            def rms_factor(b):
                pool.wait_ge(msq_ready, b + 1)
                pool.tensor_tensor(rms, rms, half_neg[:, 0:2 * JT], ALU.pow).then_inc(rms_ready, 1)

            def rstd2(n):
                pool.wait_ge(mv2_ready, n * BT + BT)
                pool.tensor_tensor(rs2[:, 0, :], mv2[:, :, 1], eps_t[:, :], ALU.add).then_inc(rs2_half, 1)
                pool.wait_ge(rs2_half, n + 1)
                pool.tensor_tensor(rs2[:, 1, :], rs2[:, 0, :], half_neg[:, 0:BT], ALU.pow).then_inc(rs2_ready, 1)

            def low_part(b, j):
                pool.wait_ge(whi_ready, b * 2 + j + 1)
                at = bass.ds(b * (2 * WSTEP) + j * WSTEP, WSTEP)
                pool.tensor_tensor(w_lo[:, at], w_stage[:, j, :], w_hi[:, at].bitcast(F32), ALU.subtract).then_inc(wlo_ready, 1)

            def body(b, half, par):
                start = isinstance(b, int) and b == 0
                if not start:
                    y2(b - 1, 1)
                pool.wait_ge(base_half, b * 2 + 2)
                pool.tensor_tensor(base[par], base[par], bc(rows[:, ROW_OPB:ROW_OPB + C], 1, JT), ALU.add).then_inc(base_ready, 1)
                if not last(b, 2):
                    low_part(b, 0)
                if not start:
                    rms_factor(b - 1)
                if not last(b, 2):
                    low_part(b, 1)
                if isinstance(b, int) and b == B - 2:
                    rstd2(0)
                y2(b, 0)

            sequences(pool, body)
            low_part(14, 0)
            low_part(14, 1)
            y2(15, 1)
            low_part(15, 0)
            low_part(15, 1)
            rms_factor(15)
            pool.sem_inc(lop_ready, 2)
            pool.wait_ge(rms_ready, B)
            barrier(pool, mamba_over)

            def hidden(q, c):
                pool.wait_ge(a_ready, q + 1)
                pool.wait_ge(s_ready, q + 1)
                pool.wait_ge(lop_ready, q + 1)
                pool.tensor_tensor(h_t[c % 2][:, 0:HS], a_t[c % 2][:, 0:HS], s_t[c % 2][:, 0:HS], ALU.mult).then_inc(hp_ready, 1)

            hidden(0, 0)

            def blk(n, par, more):
                for c in range(NC):
                    q = n * NC + c
                    if more and c == 6:
                        rstd2(n + 1)
                    if more or c + 1 < NC:
                        hidden(q + 1, c + 1)
                    pool.wait_ge(hhi_ready, q + 1)
                    pool.tensor_tensor(h_lo[c % 2][:, 0:HS], h_t[c % 2][:, 0:HS], h_hi[c % 2][:, 0:HS].bitcast(F32), ALU.subtract).then_inc(lop_ready, 1)

            blocks(pool, blk)

        @block.scalar
        def _(act):
            act.wait_ge(inw_in, 32)
            act.wait_ge(init_done, 2)
            for g in range(3):
                for pair in range(2):
                    for s in range(2):
                        k = CW[1] + KCONV * g + TAPS[1][pair][s]
                        act.activation(wnat[:, 1, 2 * g + pair, HALF * s:HALF * s + HALF], inw[:, 1, 1 + g, :],
                                       ACT.Copy, scale=cols[:, k:k + 1])
            act.activation(wnat[:, 1, 6, HALF:P], inw[:, 1, 0, :], ACT.Copy).then_inc(wnat1_ready, 1)
            for i in range(4):
                act.wait_ge(wT_ready, i + 1)
                lo, hi = 4 * i, min(4 * i + 4, 14)
                for m in range(lo, hi):
                    d, s = m // 7, m % 7
                    ins = act.activation(wp_hi[:, d, s, :], bank[i][:, (m - lo) * P:(m - lo + 1) * P],
                                         ACT.Copy, scale=cols[:, NWS[d]:NWS[d] + 1])
                ins.then_inc(wT_copied, 1)
            for n in range(NB):
                act.wait_ge(xproT_ready, n + 1)
                if n >= 2:
                    act.wait_ge(dt_ready, n - 1)
                act.activation(xT_pro[:, n % 2, :], bank[4 + n % 2][:, :], ACT.Copy).then_inc(xproT_copied, 1)
                if n == NB - 2:
                    act.wait_ge(variance_ready, 1)
                    act.activation(root, variance, ACT.Sqrt).then_inc(root_ready, 1)
            act.wait_ge(params_in, 16 * 4)
            act.activation(ea, rows[:, ROW_ALOG:ROW_ALOG + 2 * NHD], ACT.Exp).then_inc(ea_ready, 1)
            act.activation(gw_hi[:, :], gwt, ACT.Copy).then_inc(gw_ready, 1)
            act.wait_ge(mo_ready, 1)
            for d in range(2):
                ins = act.activation(mo_w[:, d, :], bank[7][:, d * P:d * P + P], ACT.Copy,
                                     scale=cols[:, GN[d]:GN[d] + 1])
            ins.then_inc(mo_copied, 1)
            act.wait_ge(abs_ready, 1)
            act.activation(sp_e, sp_abs, ACT.Exp, scale=-1.0).then_inc(e_ready, 1)
            act.wait_ge(pads_ready, 8)

            def stacks(b, par):
                act.wait_ge(t_ready, b + 1)
                f, r = stack_hi[par]
                T0, T1 = bank[4][:, 0:L], bank[4][:, L:2 * L]
                act.activation(f[0:HALF, 2:2 + L], T0[0:HALF, :], ACT.Copy).then_inc(stack_ready, 1)
                act.activation(f[HALF:P, 3:3 + L], T0[HALF:P, :], ACT.Copy).then_inc(stack_ready, 1)
                act.activation(r[HALF:P, 0:L], T1[HALF:P, :], ACT.Copy).then_inc(stack_ready, 1)
                act.activation(r[0:HALF, 0:L - 1], T1[0:HALF, 1:L], ACT.Copy).then_inc(stack_ready, 1)

            def silus(b, d):
                start = isinstance(b, int) and b == 0
                if not start:
                    act.wait_ge(y1_ready, b * 2 + d - 1)
                    act.wait_ge(xtok_ready, b * 2 + d - 1)
                    act.wait_ge(g_ready, b * 2 + d - 1)
                    act.wait_ge(y2_ready, b * 2 + d - 1)
                act.wait_ge(proj_ready, b * 4 + 2 * d + 1)
                bias = cols[:, CB[d]:CB[d] + 3]
                p0, p1 = bank[2 * d], bank[2 * d + 1]
                act.activation(xT[d], p0[:, 0:L], ACT.Silu, bias=bias[:, 0:1]).then_inc(silu_ready, 1)
                act.activation(bT[d], p0[:, L:2 * L], ACT.Silu, bias=bias[:, 1:2]).then_inc(silu_ready, 1)
                act.wait_ge(proj_ready, b * 4 + 2 * d + 2)
                act.activation(cT[d], p1[:, 0:L], ACT.Silu, bias=bias[:, 2:3]).then_inc(silu_ready, 1)
                act.activation(szT[d], p1[:, L:2 * L], ACT.Silu).then_inc(silu_ready, 1)

            def squares(b, d):
                act.wait_ge(y2_ready, b * 2 + d + 1)
                if not (isinstance(b, int) and b == 0):
                    act.wait_ge(ssq_ready, b)
                act.activation(ysqT[d], yT[d], ACT.Square).then_inc(ysq_ready, 1)

            def residual(b, half, par):
                if isinstance(b, int) and b == 0:
                    act.wait_ge(norm_ready, 1)
                act.wait_ge(x_in[par], half * 16 + 16)
                if not (isinstance(b, int) and b < 2):
                    act.wait_ge(x2_out[par], half * 16)
                for j in range(JT):
                    act.activation(base[par][:, j, :], xt[par][:, j, :], ACT.Identity, bias=c2[:, bass.ds(b * JT + j, 1)],
                                   scale=c1[:, bass.ds(b * JT + j, 1)]).then_inc(base_half, 1)

            def x3_high(n, par):
                act.wait_ge(x3T_ready, n + 1)
                act.activation(x3_hi[par][:, :], bank[x3_bank(n)][:, :], ACT.Copy).then_inc(x3hi_ready, 1)

            def x2_copy(n, par):
                act.wait_ge(x2T_ready, n + 1)
                if not (isinstance(n, int) and n == 0):
                    act.wait_ge(ob_ready, n + 1)
                act.activation(x2T[par], bank[7][:, :], ACT.Copy).then_inc(x2T_copied, 1)

            def gate_exp(n):
                act.wait_ge(logits_ready, n + 1)
                act.activation(nexp, bank[logit_bank(n)][:, 0:BT * E].rearrange("p (a b) -> p a b", a=BT), ACT.Exp, scale=-1.0).then_inc(nexp_ready, 1)

            def high_part(b, j):
                act.wait_ge(w_in[j], b * 16 + 16)
                act.activation(w_hi[:, bass.ds(b * (2 * WSTEP) + j * WSTEP, WSTEP)], w_stage[:, j, :], ACT.Copy).then_inc(whi_ready, 1)

            stacks(0, 0)
            act.wait_ge(arg_ready, 1)
            act.activation(sp_arg, sp_abs, ACT.Exp, scale=-1.0).then_inc(dec_ready, 1)
            act.wait_ge(decT_ready, 1)
            act.activation(decT, bank[7][:, L:L + P], ACT.Copy).then_inc(decT_copied, 1)

            def body(b, half, par):
                start = isinstance(b, int) and b == 0
                silus(b, 0)
                if not start:
                    squares(b - 1, 0)
                if not last(b, 1):
                    if not start:
                        act.wait_ge(proj_ready, b * 4)
                    stacks(b + 1, 1 - par)
                if not start:
                    squares(b - 1, 1)
                residual(b, half, par)
                if isinstance(b, int) and b == B - 1:
                    x3_high(0, 0)
                if not last(b, 2):
                    high_part(b, 0)
                silus(b, 1)
                if isinstance(b, int) and b == B - 1:
                    gate_exp(0)
                    act.wait_ge(proj_ready, 4 * B)
                    high_part(B - 2, 0)
                    high_part(B - 2, 1)
                if not last(b, 2):
                    high_part(b, 1)

            sequences(act, body)
            squares(15, 0)
            high_part(15, 0)
            high_part(15, 1)
            squares(15, 1)
            def rw_copy(n, par):
                act.wait_ge(rwT_ready, n + 1)
                act.activation(rwb[par], bank[7][:, :], ACT.Copy).then_inc(rwb_ready, 1)

            def silu(q, c):
                act.wait_ge(gate_ready, q + 1)
                act.activation(s_t[c % 2], bank[c % 2][:, :], ACT.Silu).then_inc(s_ready, 1)

            silu(0, 0)
            x2_copy(0, 0)
            rw_copy(0, 0)
            act.wait_ge(rwb_ready, 1)
            barrier(act, mamba_over)

            def blk(n, par, more):
                for c in range(NC):
                    q = n * NC + c
                    if more:
                        if c == 12:
                            x3_high(n + 1, 1 - par)
                        if c == 13:
                            x2_copy(n + 1, 1 - par)
                        if c == 16:
                            gate_exp(n + 1)
                        if c == 42:
                            rw_copy(n + 1, 1 - par)
                    if more or c + 1 < NC:
                        silu(q + 1, c + 1)
                    act.wait_ge(hp_ready, q + 1)
                    act.wait_ge(hv_ready, q + 1)
                    act.wait_ge(down_done, q + 1)
                    act.activation(h_hi[c % 2][:, :], h_t[c % 2], ACT.Copy).then_inc(hhi_ready, 1)

            blocks(act, blk)

        @block.vector
        def _(dve):
            links = [0]

            def link(ins):
                links[0] += 1
                ins.then_inc(link_v, 1)
                dve.wait_ge(link_v, links[0])

            factors = mean_rms.rearrange("p n k -> p (n k)")

            def normed(b, half, par):
                dve.wait_ge(x_in[par], half * 16 + 16)
                for j in range(JT):
                    src = bc(xt[par][:, j, :].rearrange("p (d c) -> p d c", d=2), 2, 2)
                    i = b * JT + j
                    dve.tensor_scalar(u2[:, j, :].rearrange("p (d r c) -> p d r c", d=2, r=2), src,
                                      factors[:, bass.ds(i * 2, 1)], factors[:, bass.ds(i * 2 + 1, 1)],
                                      ALU.subtract, ALU.mult).then_inc(u_ready, 1)

            dve.wait_ge(inw_in, 32)
            dve.wait_ge(init_done, 1)
            for g in range(3):
                for pair in range(2):
                    for s in range(2):
                        k = CW[0] + KCONV * g + TAPS[0][pair][s]
                        dve.tensor_scalar(wnat[:, 0, 2 * g + pair, HALF * s:HALF * s + HALF],
                                          inw[:, 0, 1 + g, :], cols[:, k:k + 1], None, ALU.mult)
            dve.tensor_copy(wnat[:, 0, 6, 0:HALF], inw[:, 0, 0, :]).then_inc(wnat_ready, 1)
            dve.tensor_scalar(wdt, cols[:, WDT:WDT + 2 * NHD], cols[:, NWN:NWN + 1], None, ALU.mult).then_inc(wdt_ready, 1)
            for n in range(NB + 1):
                if n < NB:
                    dve.wait_ge(x_all_in[n], 16)
                    for i in range(n * BT, n * BT + BT):
                        dve.bn_stats(stats[:, i, :], x_block(n)[:, i - n * BT, :]).then_inc(stats_ready, 1)
                if n > 0:
                    dve.wait_ge(stats_ready, n * BT)
                    for i in range(n * BT - BT, n * BT):
                        dve.bn_aggr(mv[:, i, :], stats[:, i, :]).then_inc(mv_ready, 1)
            dve.wait_ge(mv_ready, NT)
            mean, var = mv[:, :, 0], mv[:, :, 1]
            link(dve.tensor_scalar(variance[:, 0, :], var, EPS, None, ALU.add))
            dve.scalar_tensor_tensor(variance[:, 1, :], variance[:, 0, :], EPS, var, ALU.mult, ALU.add).then_inc(variance_ready, 1)
            for i in range(4):
                dve.wait_ge(wT_copied, i + 1)
                lo, hi = 4 * i, min(4 * i + 4, 14)
                for m in range(lo, hi):
                    d, s = m // 7, m % 7
                    ins = dve.scalar_tensor_tensor(wp_lo[:, d, s, :], bank[i][:, (m - lo) * P:(m - lo + 1) * P], cols[:, NWS[d]:NWS[d] + 1],
                                                   wp_hi[:, d, s, :].bitcast(F32), ALU.mult, ALU.subtract)
                ins.then_inc(wplo_ready, 1)
            dve.wait_ge(root_ready, 1)
            link(dve.reciprocal(factor, root))
            link(dve.tensor_tensor(newton, factor, factor, ALU.mult))
            link(dve.tensor_tensor(newton, newton, variance, ALU.mult))
            link(dve.tensor_scalar(newton, newton, -0.5, 1.5, ALU.mult, ALU.add))
            link(dve.tensor_tensor(factor, factor, newton, ALU.mult))
            dve.wait_ge(params_in, 16 * 4)
            dve.wait_ge(dt_ready, NB)
            nt_h = "p (n h) -> p n h"
            dtb = bc(rows[:, ROW_DTB:ROW_DTB + 2 * NHD], 1, NT)
            v3 = sp_arg.rearrange(nt_h, n=NT)
            link(dve.tensor_tensor(v3, bank[6][:, 0:P].rearrange(nt_h, n=NT), bc(factor[:, 1, :], 2, 2 * NHD), ALU.mult))
            link(dve.tensor_tensor(v3, v3, dtb, ALU.add))
            dve.scalar_tensor_tensor(sp_abs, sp_arg, -1.0, sp_arg, ALU.mult, ALU.max).then_inc(abs_ready, 1)
            dve.tensor_copy(mean_rms[:, :, 0], mean)
            link(dve.tensor_copy(mean_rms[:, :, 1], factor[:, 1, :]))
            normed(0, 0, 0)
            dve.wait_ge(e_ready, 1)
            link(dve.tensor_scalar(sp_s2, sp_e, 2.0, None, ALU.add))
            link(dve.reciprocal(sp_p, sp_s2))
            link(dve.tensor_tensor(sp_s, sp_e, sp_p, ALU.mult))
            link(dve.tensor_tensor(sp_s2, sp_s, sp_s, ALU.mult))
            link(dve.tensor_scalar(sp_p, sp_s2, 1.0 / 15, None, ALU.mult))
            for k in (13, 11, 9, 7, 5, 3):
                link(dve.scalar_tensor_tensor(sp_p, sp_p, 1.0 / k, sp_s2, ALU.add, ALU.mult))
            link(dve.scalar_tensor_tensor(sp_p, sp_p, 1.0, sp_s, ALU.add, ALU.mult))
            link(dve.tensor_scalar(sp_s, sp_arg, 0.0, None, ALU.max))
            dt_flat = dt_all.rearrange("p n h -> p (n h)")
            link(dve.scalar_tensor_tensor(dt_flat, sp_p, 2.0, sp_s, ALU.mult, ALU.add))
            dve.wait_ge(ea_ready, 1)
            dve.tensor_tensor(sp_abs.rearrange(nt_h, n=NT), dt_all, bc(ea, 1, NT), ALU.mult).then_inc(arg_ready, 1)
            link(dve.tensor_scalar(c1, factor[:, 0, :], 1.0, None, ALU.add))
            dve.scalar_tensor_tensor(c2, mean, -1.0, factor[:, 0, :], ALU.mult, ALU.mult).then_inc(norm_ready, 1)
            dve.wait_ge(gw_ready, 1)
            dve.tensor_tensor(gw_lo[:, :], gwt, gw_hi[:, :].bitcast(F32), ALU.subtract).then_inc(gw_ready, 1)

            def stack_low(b, par):
                dve.wait_ge(stack_ready, b * 4 + 4)
                fh, rh = (t[:, :].bitcast(F32) for t in stack_hi[par])
                f, r = stack_lo[par]
                T0, T1 = bank[4][:, 0:L], bank[4][:, L:2 * L]
                dve.tensor_tensor(f[0:HALF, 2:2 + L], T0[0:HALF, :], fh[0:HALF, 2:2 + L], ALU.subtract).then_inc(stacklo_ready, 1)
                dve.tensor_tensor(f[HALF:P, 3:3 + L], T0[HALF:P, :], fh[HALF:P, 3:3 + L], ALU.subtract).then_inc(stacklo_ready, 1)
                dve.tensor_tensor(r[HALF:P, 0:L], T1[HALF:P, :], rh[HALF:P, 0:L], ALU.subtract).then_inc(stacklo_ready, 1)
                dve.tensor_tensor(r[0:HALF, 0:L - 1], T1[0:HALF, 1:L], rh[0:HALF, 0:L - 1], ALU.subtract).then_inc(stacklo_ready, 1)

            def scan(b, d):
                if not (isinstance(b, int) and b == 0):
                    dve.wait_ge(y_ready, b * 2 + d - 1)
                else:
                    dve.wait_ge(pads_ready, 12)
                dve.wait_ge(decay_in[d], b * 32 + 32)
                way = slice(None, None, 1 if d == 0 else -1)
                for h in range(NHD):
                    ins = dve.tensor_tensor_scan(lmask[d][:, h, way], decay[d][:, h, way], scan_eye[:, way],
                                                 0.0, ALU.mult, ALU.add)
                ins.then_inc(l_ready, 1)

            def xdt_step(b, d):
                dve.wait_ge(xtok_ready, b * 2 + d + 1)
                if not (isinstance(b, int) and b == 0):
                    dve.wait_ge(y_ready, b * 2 + d - 1)
                dtv = dt_all.rearrange("p (b j) h -> p b j h", j=JT)[:, bass.ds(b, 1), :, NHD * d:NHD * d + NHD]
                dtv = dtv.rearrange("p o j h -> p (o j) h")
                dve.tensor_tensor(xdt[d], bank[5][:, 0:L].rearrange("p (j h c) -> p j h c", j=JT, h=NHD),
                                  bc(dtv, 3, HD), ALU.mult).then_inc(xdt_ready, 1)

            def m_step(b, d):
                dve.wait_ge(g_ready, b * 2 + d + 1)
                dve.wait_ge(l_ready, b * 2 + d + 1)
                dve.tensor_tensor(lmask[d], bc(bank[6][:, 0:LB], 1, NHD), lmask[d], ALU.mult).then_inc(m_ready, 1)

            def y1(b, d):
                dve.wait_ge(y_ready, b * 2 + d + 1)
                dve.wait_ge(silu_ready, b * 8 + 4 * d + 1)
                if not (isinstance(b, int) and b == 0):
                    dve.wait_ge(out_ready, b)
                    dve.wait_ge(ysq_ready, b * 2)
                dve.scalar_tensor_tensor(yT[d], xT[d], cols[:, DCOL[d]:DCOL[d] + 1], bank[7][:, 0:L],
                                         ALU.mult, ALU.add).then_inc(y1_ready, 1)

            def mean_square(b):
                dve.wait_ge(ssq_ready, b + 1)
                dve.wait_ge(x2_ready, b * 2)
                dve.tensor_scalar(rms, bank[7][:, L:L + 2 * JT], 1.0 / C, EPS, ALU.mult, ALU.add).then_inc(msq_ready, 1)

            def x2_step(b, par):
                dve.wait_ge(out_ready, b + 1)
                dve.wait_ge(rms_ready, b + 1)
                dve.wait_ge(base_ready, b + 1)
                for d in range(2):
                    for j in range(JT):
                        m = d * JT + j
                        dve.scalar_tensor_tensor(base[par][:, j, :], bank[4][:, m * P:m * P + P], rms[:, m:m + 1],
                                                 base[par][:, j, :], ALU.mult, ALU.add)\
                           .then_inc(x2_half if d == 0 else x2_ready, 1)
                    if d == 0:
                        dve.wait_ge(x2_half, b * 2 + 2)

            ROUTE = 34
            g8 = "p t (g e) -> p (t g) e"

            def route(n, piece):
                r = n * ROUTE

                def step(k, *ins):
                    if k > 1:
                        dve.wait_ge(route_link, r + k - 1)
                    op, *operands = ins
                    op(*operands).then_inc(route_link, 1)

                ch = choice.rearrange(g8, g=NG)
                tt, ts = dve.tensor_tensor, dve.tensor_scalar
                if piece == 0:
                    dve.wait_ge(nexp_ready, n + 1)
                    step(1, ts, choice, nexp, 1.0, None, ALU.add)
                elif piece <= BT:
                    t = piece - 1
                    step(2 + t, dve.reciprocal, scores[:, t, :], choice[:, t, :])
                elif piece == 5:
                    step(6, tt, choice, scores, bc(rows[:, ROW_GB:ROW_GB + E], 1, BT), ALU.add)
                elif piece == 6:
                    step(7, tt, t1h, ch[:, :, 0:4], ch[:, :, 4:8], ALU.max)
                    step(8, tt, t1l, ch[:, :, 0:4], ch[:, :, 4:8], ALU.min)
                elif piece == 7:
                    step(9, tt, t2h, t1h[:, :, 0:2], t1h[:, :, 2:4], ALU.max)
                    step(10, tt, t2a, t1h[:, :, 0:2], t1h[:, :, 2:4], ALU.min)
                elif piece == 8:
                    step(11, tt, t2b, t1l[:, :, 0:2], t1l[:, :, 2:4], ALU.max)
                    step(12, tt, t2l, t2a, t2b, ALU.max)
                elif piece == 9:
                    step(13, tt, t3h, t2h[:, :, 0:1], t2h[:, :, 1:2], ALU.max)
                    step(14, tt, t3a, t2h[:, :, 0:1], t2h[:, :, 1:2], ALU.min)
                    step(15, tt, t3b, t2l[:, :, 0:1], t2l[:, :, 1:2], ALU.max)
                elif piece == 10:
                    step(16, tt, t3b, t3a, t3b, ALU.max)
                    step(17, tt, gs, t3h, t3b, ALU.add)
                elif piece in (11, 12):
                    gsv = gs.rearrange("p (t g) o -> p t (g o)", t=BT)
                    other, own = bc(gsv, 2, NG), bc(gsv, 3, NG)
                    if piece == 11:
                        step(18, tt, cmp1.rearrange("p t (g o) -> p t g o", g=NG), other, own, ALU.is_gt)
                    else:
                        step(19, tt, cmp2.rearrange("p t (g o) -> p t g o", g=NG), other, own, ALU.is_equal)
                elif piece == 13:
                    step(20, tt, cmp2, cmp2, bc(tri[:, :], 1, BT), ALU.mult)
                elif piece == 14:
                    step(21, tt, cmp1, cmp1, cmp2, ALU.add)
                elif piece == 15:
                    step(22, dve.tensor_reduce, rank, cmp1.rearrange("p t (g o) -> p t g o", g=NG), X, ALU.add)
                    step(23, ts, rank, rank, TOPG - 0.5, None, ALU.is_lt)
                elif piece == 16:
                    gm = bc(rank.rearrange("p t g -> p (t g)"), 2, EPG)
                    step(24, tt, masked.rearrange(g8, g=NG), ch, gm, ALU.mult)
                    dve.wait_ge(route_link, r + 24)
                elif piece == 17:
                    for t in range(BT):
                        ins = dve.max(m8[:, t, :], masked[:, t, :])
                    ins.then_inc(route_link, 1)
                    dve.wait_ge(route_link, r + 25)
                elif piece == 18:
                    for t in range(BT):
                        ins = dve.match_replace(repl[:, t, :], m8[:, t, :], masked[:, t, :], LOWEST)
                    ins.then_inc(route_link, 1)
                elif piece == 19:
                    step(27, tt, wsel, repl, masked, ALU.not_equal)
                elif piece == 20:
                    step(28, tt, wsel, wsel, scores, ALU.mult)
                elif piece == 21:
                    step(29, dve.tensor_reduce, den, wsel, X, ALU.add)
                    step(30, ts, den, den, 1e-20, None, ALU.add)
                    step(31, dve.reciprocal, den, den)
                elif piece == 22:
                    step(32, ts, den, den, SCALE, None, ALU.mult)
                    step(33, tt, wsel, wsel, bc(den, 2, E), ALU.mult)
                elif piece == 23:
                    if not (isinstance(n, int) and n == 0):
                        dve.wait_ge(rwT_ready, n)
                    step(34, dve.tensor_copy, rwp[:, :, 0:E], wsel)
                    dve.tensor_copy(rwp[:, :, E:2 * E], wsel).then_inc(rwp_ready, 1)

            def stats2(n, t0, t1):
                if t0 == 0:
                    dve.wait_ge(x2_in, n * 16 + 16)
                for t in range(t0, t1):
                    dve.bn_stats(st2[:, t, :], x2t[:, t, :]).then_inc(stat2_ready, 1)

            def aggr2(n):
                for t in range(BT):
                    dve.bn_aggr(mv2[:, t, :], st2[:, t, :]).then_inc(mv2_ready, 1)

            def x3_step(n, t0, t1):
                if t0 == 0:
                    dve.wait_ge(rs2_ready, n + 1)
                for t in range(t0, t1):
                    dve.tensor_scalar(x3t[:, t, :], x2t[:, t, :], mv2[:, t, 0:1], rs2[:, 1, t:t + 1],
                                      ALU.subtract, ALU.mult).then_inc(x3_ready, 1)

            def x3_low(n, par):
                dve.wait_ge(x3hi_ready, n + 1)
                dve.tensor_tensor(x3_lo[par][:, :], bank[x3_bank(n)][:, :], x3_hi[par][:, :].bitcast(F32), ALU.subtract).then_inc(x3lo_ready, 1)

            stack_low(0, 0)
            normed(1, 0, 1)

            def body(b, half, par):
                start = isinstance(b, int) and b == 0
                final = isinstance(b, int) and b == B - 1
                before = isinstance(b, int) and b == B - 2
                scan(b, 0)
                if start:
                    stack_low(1, 1)
                if final:
                    x3_step(0, 0, BT)
                if not start:
                    y1(b - 1, 1)
                scan(b, 1)
                if final:
                    x3_low(0, 0)
                if not (start or final):
                    stack_low(b + 1, 1 - par)
                xdt_step(b, 0)
                m_step(b, 0)
                if not start:
                    mean_square(b - 1)
                if final:
                    for piece in range(2):
                        route(0, piece)
                xdt_step(b, 1)
                if final:
                    for piece in range(2, 4):
                        route(0, piece)
                m_step(b, 1)
                if final:
                    for piece in range(4, 7):
                        route(0, piece)
                    y1(b, 0)
                if not start:
                    x2_step(b - 1, 1 - par)
                if before:
                    stats2(0, 0, BT)
                    dve.wait_ge(stat2_ready, BT)
                    aggr2(0)
                if not final:
                    y1(b, 0)
                if not last(b, 2):
                    dve.wait_ge(t_ready, b + 2)
                    normed(b + 2, half + 1, par)

            sequences(dve, body)
            for piece in range(7, PIECES):
                if piece == 11:
                    y1(15, 1)
                if piece == 19:
                    mean_square(15)
                route(0, piece)
            x2_step(15, 1)
            dve.sem_inc(ob_ready, 2)
            dve.sem_inc(lov_ready, 2)
            dve.wait_ge(x2_ready, 2 * B)
            barrier(dve, mamba_over)

            def weigh(n, q, c, par):
                dve.wait_ge(up_ready, q + 1)
                if c % NC < RC:
                    if c % NC == 0:
                        dve.wait_ge(rwb_ready, n + 1)
                    dve.tensor_tensor(a_t[c % 2], bank[2 + c % 2][:, :], rwb[par], ALU.mult).then_inc(a_ready, 1)
                else:
                    dve.tensor_copy(a_t[c % 2], bank[2 + c % 2][:, :]).then_inc(a_ready, 1)

            def hidden(q, c):
                dve.wait_ge(a_ready, q + 1)
                dve.wait_ge(s_ready, q + 1)
                dve.wait_ge(lov_ready, q + 1)
                dve.tensor_tensor(h_t[c % 2][:, HS:TB], a_t[c % 2][:, HS:TB], s_t[c % 2][:, HS:TB], ALU.mult).then_inc(hv_ready, 1)

            weigh(0, 0, 0, 0)
            weigh(0, 1, 1, 0)
            hidden(0, 0)

            def step(n, c, par, more):
                q = n * NC + c
                if more:
                    if c in (3, 4):
                        stats2(n + 1, 2 * (c - 3), 2 * (c - 3) + 2)
                    if c == 5:
                        dve.wait_ge(stat2_ready, n * BT + 2 * BT)
                    if c in (8, 9):
                        x3_step(n + 1, 2 * (c - 8), 2 * (c - 8) + 2)
                    if c == 14:
                        x3_low(n + 1, 1 - par)
                    if 17 <= c < 17 + PIECES:
                        route(n + 1, c - 17)
                if more or c + 1 < NC:
                    hidden(q + 1, c + 1)
                if more and c == 5:
                    aggr2(n + 1)
                dve.wait_ge(hhi_ready, q + 1)
                dve.tensor_tensor(h_lo[c % 2][:, HS:TB], h_t[c % 2][:, HS:TB], h_hi[c % 2][:, HS:TB].bitcast(F32), ALU.subtract).then_inc(lov_ready, 1)
                if more or c + 2 < NC:
                    dve.wait_ge(hp_ready, q + 1)
                    if c + 2 < NC:
                        weigh(n, q + 2, c + 2, par)
                    else:
                        weigh(n + 1, q + 2, c + 2, 1 - par)

            for c in range(LAG):
                step(0, c, 0, True)

            def blk(n, par, more):
                for c in range(LAG, NC + LAG if more else NC):
                    step(n, c, par, more)
                dve.wait_ge(down_done, n * NC + NC + 2)
                dve.wait_ge(x2T_copied, n + 1)
                dve.wait_ge(out_sent, n * 16 + 16)
                dve.tensor_tensor(ob, bank[4 + par][:, :], x2T[par], ALU.add).then_inc(ob_ready, 1)

            blocks(dve, blk)

        @block.tensor
        def _(pe):
            pe.wait_ge(eye_in, 16)
            for i in range(4):
                lo, hi = 4 * i, min(4 * i + 4, 14)
                pe.wait_ge(wnat_ready, 1)
                if hi > 7:
                    pe.wait_ge(wnat1_ready, 1)
                for m in range(lo, hi):
                    ins = pe.transpose(bank[i][:, (m - lo) * P:(m - lo + 1) * P], wnat[:, m // 7, m % 7, :], ident)
                ins.then_inc(wT_ready, 1)
            pe.wait_ge(wdt_ready, 1)
            for n in range(NB + 1):
                if n < NB:
                    pe.wait_ge(centered, n + 1)
                    if n >= 2:
                        pe.wait_ge(xproT_copied, n - 1)
                    for j in range(BT):
                        ins = pe.transpose(bank[4 + n % 2][:, j * P:j * P + P], x_block(n)[:, j, :], ident)
                    ins.then_inc(xproT_ready, 1)
                if n > 0:
                    pe.wait_ge(xproT_copied, n)
                    for j in range(BT):
                        i = ((n - 1) * BT + j) * 2 * NHD
                        ins = pe.matmul(bank[6][:, i:i + 2 * NHD], xT_pro[:, (n - 1) % 2, j * P:j * P + P], wdt, start=True, stop=True)
                    ins.then_inc(dt_ready, 1)
            pe.wait_ge(params_in, 16 * 4)
            for d in range(2):
                ins = pe.matmul(bank[7][:, d * P:d * P + P], mo_sb[0:HALF, 2 * d, :], mo_sb[0:HALF, 2 * d + 1, :], start=True, stop=True)
            ins.then_inc(mo_ready, 1)

            def decays_turned():
                pe.wait_ge(dec_ready, 1)
                pe.transpose(bank[7][:, L:L + P], sp_arg, ident).then_inc(decT_ready, 1)

            def tokensT(b):
                pe.wait_ge(u_ready, b * 2 + 2)
                for d in range(2):
                    for j in range(JT):
                        ins = pe.transpose(bank[4][:, d * L + j * P:d * L + j * P + P],
                                           u2[:, j, d * C:d * C + C], ident)
                ins.then_inc(t_ready, 1)

            def three(o, wk, hi, lo, first, final):
                pe.matmul(o, wk[0], hi, start=first, stop=False)
                pe.matmul(o, wk[1], hi, start=False, stop=False)
                return pe.matmul(o, wk[0], lo, start=False, stop=final)

            def proj(b, d, par):
                pe.wait_ge(stacklo_ready, b * 4 + 4)
                if not (isinstance(b, int) and b == 0):
                    pe.wait_ge(silu_ready, b * 8 + 4 * d - 4)
                elif d == 0:
                    pe.wait_ge(wplo_ready, 4)
                hi, lo = stack_hi[par][d], stack_lo[par][d]
                at_near, at_far = (2, 0) if d == 0 else (0, 2)
                for half in range(2):
                    for g in range(2):
                        w = 2 * half + g
                        o = bank[2 * d + half][:, g * L:g * L + L]
                        for k, at in ((2 * w, at_near), (2 * w + 1, at_far))[:2 if w < 3 else 1]:
                            ins = three(o, (wp_hi[:, d, k, :], wp_lo[:, d, k, :]), hi[:, at:at + L], lo[:, at:at + L],
                                        at == at_near, at == at_far or w == 3)
                    ins.then_inc(proj_ready, 1)

            def scores_of(b, d):
                pe.wait_ge(silu_ready, b * 8 + 4 * d + 3)
                if d or not (isinstance(b, int) and b == 0):
                    pe.wait_ge(m_ready, b * 2 + d)
                    pe.wait_ge(xdt_ready, b * 2 + d)
                G = bank[6]
                for j in range(JT):
                    ins = pe.transpose(bank[5][:, j * P:j * P + P], xT[d][:, j * P:j * P + P], ident)
                ins.then_inc(xtok_ready, 1)
                if d == 0:
                    pe.matmul(G[:, 0:L], bT[d][:, 0:P], cT[d][:, 0:L], start=True, stop=True)
                    ins = pe.matmul(G[:, L:LB], bT[d][:, P:L], cT[d][:, P:L], start=True, stop=True)
                else:
                    pe.matmul(G[:, 0:P], bT[d][:, 0:P], cT[d][:, 0:P], start=True, stop=True)
                    ins = pe.matmul(G[:, P:LB], bT[d][:, P:L], cT[d][:, 0:L], start=True, stop=True)
                ins.then_inc(g_ready, 1)

            def y_of(b, d):
                pe.wait_ge(m_ready, b * 2 + d + 1)
                pe.wait_ge(xdt_ready, b * 2 + d + 1)
                if d or not (isinstance(b, int) and b == 0):
                    pe.wait_ge(y1_ready, b * 2 + d)
                if not (isinstance(b, int) and b == 0):
                    pe.wait_ge(msq_ready, b)
                for h in range(NHD):
                    o = bank[7][HD * h:HD * h + HD, :]
                    m = lmask[d][:, h, :]
                    src, one, both = (0, 0, P) if d == 0 else (1, P, 0)
                    m0 = m[:, 0:L] if d == 0 else m[:, P:LB]
                    m1 = m[:, L:LB] if d == 0 else m[:, 0:P]
                    pe.matmul(o[:, one:one + P], xdt[d][:, src, h, :], m0[:, one:one + P], start=True, stop=True)
                    pe.matmul(o[:, both:both + P], xdt[d][:, src, h, :], m0[:, both:both + P], start=True, stop=False)
                    ins = pe.matmul(o[:, both:both + P], xdt[d][:, 1 - src, h, :], m1, start=False, stop=True)
                ins.then_inc(y_ready, 1)

            def out_of(b):
                pe.wait_ge(y2_ready, b * 2 + 2)
                pe.wait_ge(ysq_ready, b * 2 + 2)
                for d in range(2):
                    for j in range(JT):
                        m = d * JT + j
                        ins = pe.matmul(bank[7][:, L + m:L + m + 1], ysqT[d][:, j * P:j * P + P], ones[:, :], start=True, stop=True)
                ins.then_inc(ssq_ready, 1)
                if not (isinstance(b, int) and b == 0):
                    pe.wait_ge(x2_ready, b * 2)
                if isinstance(b, int) and b == B - 2:
                    pe.wait_ge(x3lo_ready, 1)
                if not last(b, 2):
                    pe.wait_ge(stacklo_ready, b * 4 + 12)
                for d in range(2):
                    for j in range(JT):
                        m = d * JT + j
                        ins = pe.matmul(bank[4][:, m * P:m * P + P], yT[d][:, j * P:j * P + P], mo_w[:, d, :], start=True, stop=True)
                ins.then_inc(out_ready, 1)

            tokensT(0)
            decays_turned()

            def turn_x2(n):
                pe.wait_ge(x2_in, n * 16 + 16)
                if not (isinstance(n, int) and n == 0):
                    pe.wait_ge(rwb_ready, n)
                for t in range(BT):
                    ins = pe.transpose(bank[7][:, t * P:t * P + P], x2t[:, t, :], ident)
                ins.then_inc(x2T_ready, 1)

            def turn_x3(n):
                pe.wait_ge(x3_ready, n * BT + BT)
                if not (isinstance(n, int) and n == 0):
                    pe.wait_ge(nexp_ready, n)
                for t in range(BT):
                    ins = pe.transpose(bank[x3_bank(n)][:, t * P:t * P + P], x3t[:, t, :], ident)
                ins.then_inc(x3T_ready, 1)

            def logits(n, par):
                pe.wait_ge(x3lo_ready, n + 1)
                pe.wait_ge(gw_ready, 2)
                for t in range(BT):
                    o = bank[logit_bank(n)][:, t * E:t * E + E]
                    hi, lo = x3_hi[par][:, t * P:t * P + P], x3_lo[par][:, t * P:t * P + P]
                    pe.matmul(o, hi, gw_hi[:, :], start=True, stop=False)
                    pe.matmul(o, lo, gw_hi[:, :], start=False, stop=False)
                    ins = pe.matmul(o, hi, gw_lo[:, :], start=False, stop=True)
                ins.then_inc(logits_ready, 1)

            def body(b, half, par):
                start = isinstance(b, int) and b == 0
                proj(b, 0, par)
                if not start:
                    y_of(b - 1, 1)
                if not last(b, 1):
                    if not start:
                        pe.wait_ge(x2_ready, b * 2 - 2)
                    pe.wait_ge(stacklo_ready, b * 4 + 4)
                    tokensT(b + 1)
                if isinstance(b, int) and b == B - 1:
                    pe.wait_ge(x2_ready, 2 * (B - 2))
                    turn_x3(0)
                proj(b, 1, par)
                if isinstance(b, int) and b == B - 1:
                    pe.wait_ge(silu_ready, b * 8 + 4)
                    logits(0, 0)
                scores_of(b, 0)
                if not start:
                    out_of(b - 1)
                scores_of(b, 1)
                y_of(b, 0)

            sequences(pe, body)
            y_of(15, 1)
            def w(kind, c):
                at = (kind * NC + c) * P
                return w_hi[:, at:at + P], w_lo[:, at:at + P]

            def turn_rw(n):
                pe.wait_ge(rwp_ready, n + 1)
                pe.wait_ge(x2T_copied, n + 1)
                for t in range(BT):
                    ins = pe.transpose(bank[7][:, t * P:t * P + P], rwp[:, t, :], ident)
                ins.then_inc(rwT_ready, 1)

            def gate_up(c, odd, par):
                hi, lo = x3_hi[par][:, :], x3_lo[par][:, :]
                three(bank[2 + odd][:, :], w(1, c), hi, lo, True, True).then_inc(up_ready, 1)
                three(bank[odd][:, :], w(0, c), hi, lo, True, True).then_inc(gate_ready, 1)

            pe.wait_ge(silu_ready, 8 * B)
            pe.wait_ge(nexp_ready, 1)
            gate_up(0, 0, 0)
            gate_up(1, 1, 0)
            out_of(15)
            pe.wait_ge(msq_ready, B)
            turn_x2(0)
            turn_rw(0)
            pe.wait_ge(whi_ready, 2 * B)
            pe.wait_ge(wlo_ready, 2 * B)
            pe.sem_inc(down_done, 2)
            pe.wait_ge(rwT_ready, 1)
            barrier(pe, mamba_over)

            pe.wait_ge(s_ready, 1)
            pe.wait_ge(a_ready, 1)
            gate_up(2, 0, 0)

            def blk(n, par, more):
                for c in range(NC):
                    q = n * NC + c
                    if more:
                        if c == 10:
                            turn_x2(n + 1)
                            turn_x3(n + 1)
                        if c == 14:
                            logits(n + 1, 1 - par)
                        if c == 40:
                            turn_rw(n + 1)
                    if more or c + LAG < NC:
                        pe.wait_ge(s_ready, q + 2)
                        pe.wait_ge(a_ready, q + 2)
                        gate_up((c + LAG) % NC, (c + LAG) % 2, par if c + LAG < NC else 1 - par)
                    if c == 0:
                        pe.wait_ge(ob_ready, n + 1)
                    pe.wait_ge(lop_ready, q + 3)
                    pe.wait_ge(lov_ready, q + 3)
                    three(bank[4 + par][:, :], w(2, c), h_hi[c % 2][:, :], h_lo[c % 2][:, :],
                          c == 0, c == NC - 1).then_inc(down_done, 1)

            blocks(pe, blk)


def kernel(**inputs):
    import numpy as np
    import concourse.bacc as bacc
    from concourse.bass_utils import run_bass_kernel_spmd as run

    a = {k: np.asarray(v) for k, v in inputs.items()}

    def at(name):
        return a["L0_attn_" + name]

    f32 = np.float32
    cols = np.zeros((P, NCOL), f32)
    rows = np.zeros((1, NROW), f32)
    inw = np.zeros((P, 2, 4, HALF), f32)
    mo = np.zeros((HALF, 4, P), f32)
    for d, p in enumerate(("f_", "b_")):
        cols[:, CW[d]:CW[d] + 12] = at(p + "conv_w").reshape(3, P, KCONV).transpose(1, 0, 2).reshape(P, 12)
        cols[:, CB[d]:CB[d] + 3] = at(p + "conv_b").reshape(3, P).T
        own = slice(HALF * d, HALF * d + HALF)
        cols[:HALF, NWS[d]] = at("norm_w")[own]
        cols[HALF:, NWS[d]] = at("norm_w")[own]
        for h in range(NHD):
            cols[HD * h:HD * h + HD, DCOL[d]] = at(p + "D")[h]
        cols[:, GN[d]] = at(p + "gnorm_w")
        cols[own, WDT + NHD * d:WDT + NHD * d + NHD] = at(p + "in_w")[4 * P:, :].T
        inw[:, d] = at(p + "in_w")[:4 * P].reshape(4, P, HALF).transpose(1, 0, 2)
        rows[0, ROW_DTB + NHD * d:ROW_DTB + NHD * d + NHD] = at(p + "dt_bias")
        rows[0, ROW_ALOG + NHD * d:ROW_ALOG + NHD * d + NHD] = at(p + "A_log")
        mo[:, 2 * d] = at(p + "outp_w")
        mo[:, 2 * d + 1] = at("op_w").T[own]
    cols[:, NWN] = at("norm_w")
    rows[0, ROW_OPB:ROW_OPB + C] = at("op_b")
    rows[0, ROW_GB:ROW_GB + E] = a["L0_ffn_gate_bias"]

    wall = np.zeros((P, 3, NC * P), f32)
    for k, (routed, shared) in enumerate((("Wg", "Sg"), ("Wu", "Su"))):
        wall[:, k, :E * I] = a["L0_ffn_" + routed].transpose(2, 1, 0).reshape(C, I * E)
        wall[:, k, E * I:E * I + SI] = a["L0_ffn_" + shared].T
    down = np.zeros((NC * P, C), f32)
    down[:E * I] = a["L0_ffn_Wd"].transpose(2, 0, 1).reshape(I * E, C)
    down[E * I:E * I + SI] = a["L0_ffn_Sd"].T
    wall[:, 2] = down.reshape(NC, P, C).transpose(1, 0, 2).reshape(P, NC * C)

    const = np.zeros((P, NK), f32)
    const[:, K_SCAN:K_SCAN + P] = np.eye(P, dtype=f32)
    const[:, K_SCAN + L:K_SCAN + LB] = np.eye(P, dtype=f32)
    const[:, K_TRI:NK] = np.tril(np.ones((NG, NG), f32), -1).reshape(1, NG * NG)

    arrays = {
        "x": np.ascontiguousarray(at("x")).reshape(T, C),
        "cols": cols, "rows": rows, "inw": inw, "mo": mo,
        "gwt": np.ascontiguousarray(a["L0_ffn_gate_w"].T),
        "wall": wall.reshape(P, WCOLS), "const": const,
    }
    nc = bacc.Bacc("TRN2", target_bir_lowering=False, num_devices=1)
    args = [nc.dram_tensor("in_" + k, v.shape, mybir.dt.from_np(v.dtype), kind="ExternalInput").ap() for k, v in arrays.items()]
    args.append(nc.dram_tensor("out_0", (C, T), F32, kind="ExternalOutput").ap())
    bidirectional_mamba_moe(nc, *args)
    r = run(nc, [{"in_" + k: v for k, v in arrays.items()}], core_ids=[0])
    return np.ascontiguousarray(r.results[0]["out_0"].T).reshape(B, L, C)
```
